# Optimizing a Trainium2 kernel written in Bass

```python
import numpy as np
import jax
import jax.numpy as jnp

def _softmax(x, axis=-1):
    return jax.nn.softmax(x, axis=axis)

def _gelu(x):
    return jax.nn.gelu(x, approximate=True)

def _silu(x):
    return jax.nn.silu(x)

def _sigmoid(x):
    return jax.nn.sigmoid(x)

def _layernorm(x, axis=-1, eps=1e-05):
    m = jnp.mean(x, axis=axis, keepdims=True)
    v = jnp.var(x, axis=axis, keepdims=True)
    return (x - m) / jnp.sqrt(v + eps)

def _scatter_add(tgt, idx, src, axis=0):
    return tgt.at[idx].add(src)

def _segment_sum(src, seg, n):
    return jax.ops.segment_sum(src, seg, n)
kernel_name = 'mk_adj_resnorm_d1_adj_r2_25e19c'

def setup_inputs(seed: int=0):
    np.random.seed(seed)
    _w = jnp.asarray

    def _rec_inputs():
        import jax
        import jax.numpy as jnp
        _gk = jax.random.key(seed)
        x = 7.22e-05 + 1 * jax.random.normal(jax.random.fold_in(_gk, 1), (8, 1024, 256), jnp.float32)
        _a = jax.random.bernoulli(jax.random.fold_in(_gk, 2), 0.015625, (8, 1024, 1024))
        _a = jnp.logical_or(_a, jnp.swapaxes(_a, -1, -2))
        _a = jnp.logical_or(_a, jnp.eye(1024, dtype=bool))
        _af = _a.astype(jnp.float32)
        _af = _af * jax.random.uniform(jax.random.fold_in(_gk, 3), (8, 1024, 1024), jnp.float32, 0.05, 1)
        adj = _af
        return (x, adj)
    x, adj = _rec_inputs()

    def _L0_gnn_setup():
        import jax, jax.numpy as jnp
        import numpy as np
        EPS_LN = 1e-05

        def hypergraph_conv(x, adj, W, b):
            N, C, _ = adj.shape
            H = (adj != 0).astype(x.dtype)
            w = adj.reshape(N, -1)[:, :C]
            xw = jnp.einsum('ncd,hd->nch', x, W)
            Dn = jnp.einsum('nce,ne->nc', H, w)
            Dn = jnp.where(Dn > 0, 1.0 / Dn, 0.0)
            Be = H.sum(axis=1)
            Be = jnp.where(Be > 0, 1.0 / Be, 0.0)
            m = Be[:, :, None] * jnp.einsum('nce,nch->neh', H, xw)
            out = Dn[:, :, None] * jnp.einsum('nce,neh->nch', H, m)
            return out + b

        def layer_norm(x, g, b):
            mu = jnp.mean(x, axis=-1, keepdims=True)
            var = jnp.var(x, axis=-1, keepdims=True)
            return (x - mu) * jax.lax.rsqrt(var + EPS_LN) * g + b
        key = jax.random.key(seed)
        ks = jax.random.split(key, 4)
        N, C, Din, Dh, Dout = (16, 512, 256, 512, 256)
        x = jax.random.normal(ks[0], (N, C, Din), dtype=jnp.float32)
        adj = jax.random.uniform(ks[1], (N, C, C), dtype=jnp.float32, minval=0.1, maxval=1.0)
        W1 = jax.random.normal(ks[2], (Dh, Din), dtype=jnp.float32) * (1.0 / np.sqrt(Din))
        b1 = jnp.zeros((Dh,), dtype=jnp.float32)
        gamma = jnp.ones((Dh,), dtype=jnp.float32)
        beta = jnp.zeros((Dh,), dtype=jnp.float32)
        W2 = jax.random.normal(ks[3], (Dout, Dh), dtype=jnp.float32) * (1.0 / np.sqrt(Dh))
        b2 = jnp.zeros((Dout,), dtype=jnp.float32)
        return {'x': x, 'adj': adj, 'W1': W1, 'b1': b1, 'gamma': gamma, 'beta': beta, 'W2': W2, 'b2': b2}
    _L0_gnn_all = _L0_gnn_setup()
    _L0_gnn_in = {k: v for k, v in _L0_gnn_all.items() if k in ('W1', 'b1', 'gamma', 'beta', 'W2', 'b2')}
    del _L0_gnn_all
    return {'x': x, 'adj': adj, 'L0_gnn_W1': _L0_gnn_in['W1'], 'L0_gnn_b1': _L0_gnn_in['b1'], 'L0_gnn_gamma': _L0_gnn_in['gamma'], 'L0_gnn_beta': _L0_gnn_in['beta'], 'L0_gnn_W2': _L0_gnn_in['W2'], 'L0_gnn_b2': _L0_gnn_in['b2']}

def reference(x, adj, L0_gnn_W1, L0_gnn_b1, L0_gnn_gamma, L0_gnn_beta, L0_gnn_W2, L0_gnn_b2):
    import jax
    import jax.numpy as jnp

    def _L0_gnn_ref(x, adj, W1, b1, gamma, beta, W2, b2):
        import jax, jax.numpy as jnp
        import numpy as np
        EPS_LN = 1e-05

        def hypergraph_conv(x, adj, W, b):
            N, C, _ = adj.shape
            H = (adj != 0).astype(x.dtype)
            w = adj.reshape(N, -1)[:, :C]
            xw = jnp.einsum('ncd,hd->nch', x, W)
            Dn = jnp.einsum('nce,ne->nc', H, w)
            Dn = jnp.where(Dn > 0, 1.0 / Dn, 0.0)
            Be = H.sum(axis=1)
            Be = jnp.where(Be > 0, 1.0 / Be, 0.0)
            m = Be[:, :, None] * jnp.einsum('nce,nch->neh', H, xw)
            out = Dn[:, :, None] * jnp.einsum('nce,neh->nch', H, m)
            return out + b

        def layer_norm(x, g, b):
            mu = jnp.mean(x, axis=-1, keepdims=True)
            var = jnp.var(x, axis=-1, keepdims=True)
            return (x - mu) * jax.lax.rsqrt(var + EPS_LN) * g + b
        h = jax.nn.relu(hypergraph_conv(x, adj, W1, b1))
        h = layer_norm(h, gamma, beta)
        y = hypergraph_conv(h, adj, W2, b2)
        return y + x
    x = _layernorm(x + _L0_gnn_ref(x, adj, L0_gnn_W1, L0_gnn_b1, L0_gnn_gamma, L0_gnn_beta, L0_gnn_W2, L0_gnn_b2), axis=-1)
    return x

_drawn_inputs = setup_inputs


def setup_inputs(seed=0):
    import zlib

    import numpy as np

    out = dict(_drawn_inputs(seed))
    spreads = {'L0_gnn_b1': (0.0, 0.1),
     'L0_gnn_gamma': (1.0, 0.2),
     'L0_gnn_beta': (0.0, 0.1),
     'L0_gnn_b2': (0.0, 0.1)}
    factors = {}
    for name, (base, spread) in spreads.items():
        noise = np.random.default_rng([zlib.crc32(name.encode()), seed]).standard_normal(out[name].shape)
        drawn = base * np.exp(spread * noise) if base else spread * noise
        out[name] = jnp.asarray(drawn.astype(out[name].dtype))
    for name, factor in factors.items():
        out[name] = (out[name] * factor).astype(out[name].dtype)
    return out
```

```python
from contextlib import ExitStack

import concourse.bass as bass
from concourse import mybir

P = 128
F32 = mybir.dt.float32
F32R = mybir.dt.float32r
ALU = mybir.AluOpType
ACT = mybir.ActivationFunctionType
EPS = 1e-5
SLOTS = 4
BANK = 512


def graph_kernel(nc: bass.Bass, x, adj, w1t, b1, gamma, beta, w2t, b2, out):
    N, C, D = x.shape
    DH = w1t.shape[1]
    K = C // P
    DB = D // P
    HB = DH // P
    CH = C // BANK
    PAIRS = K // 2
    assert C == K * P and D * 2 == BANK and DH == BANK and K == 8 and SLOTS * 2 == K and N >= 3

    adj_rows = adj.rearrange("n (p k) e -> n p k e", k=K)
    x_rows = x.rearrange("n (p k) d -> n p k d", k=K)
    out_rows = out.rearrange("n (p k) d -> n p k d", k=K)

    with ExitStack() as ctx:
        def sb(name, shape, dt=F32):
            return ctx.enter_context(nc.sbuf_tensor(name, shape, dt))

        def sem(name):
            return ctx.enter_context(nc.semaphore(name))

        adj_sb = sb("adj_sb", [P, SLOTS, C])
        H = sb("H", [P, K, C], F32R)
        HT = sb("HT", [P, K, C], F32R)
        x_sb = sb("x_sb", [P, K, D])
        resid = sb("resid", [P, K, D])
        feat = sb("feat", [P, K, 2 * D], F32R)
        mid = sb("mid", [P, K, 2 * D], F32R)
        vT = sb("vT", [P, 2, DB, C], F32R)
        hid = sb("hid", [P, K, DH])
        hidT = sb("hidT", [P, 2, 2, HB, P], F32R)
        w1p = sb("w1p", [P, 2, DB, DH], F32R)
        w2p = sb("w2p", [P, HB, 2 * D], F32R)
        w_row = sb("w_row", [P, C])
        b1_row = sb("b1_row", [P, DH])
        b2_row = sb("b2_row", [P, D])
        bw_row = sb("bw_row", [P, D])
        ident = sb("ident", [P, P])
        scaled_lo = sb("scaled_lo", [P, 2, D])
        add_lo = sb("add_lo", [P, 2, D])
        whole = sb("whole", [P, 2, D])
        y_sb = sb("y_sb", [P, 4, D])
        gcol = sb("gcol", [P, HB])
        bcol = sb("bcol", [P, HB])
        half = sb("half", [P, 2])
        count = sb("count", [P, K, CH])
        count1 = sb("count1", [P, K])
        binv = sb("binv", [P, K])
        dsum = sb("dsum", [P, K])
        dsafe = sb("dsafe", [P, K])
        drec = sb("drec", [P, K])
        dinv = sb("dinv", [P, K])
        stats = sb("stats", [P, K, 6])
        mv = sb("mv", [P, K, 2])
        veps = sb("veps", [P, K])
        rstd = sb("rstd", [P, K])
        stats2 = sb("stats2", [P, K, 6])
        mv2 = sb("mv2", [P, K, 2])
        veps2 = sb("veps2", [P, K])
        rstd2 = sb("rstd2", [P, K])
        banks = [ctx.enter_context(nc.psum_tensor(f"bank{i}", [P, BANK], F32)) for i in range(8)]

        w1_raw = resid[:, 0:4, :].rearrange("p a d -> p (a d)").rearrange("p (b h) -> p b h", b=DB)
        w2_raw = resid[:, 4:8, :]
        beta_cols = hid[:, 0, :].rearrange("p (b m) -> p b m", b=HB)
        ssum = hid[:, 0:K // 2, :].rearrange("p a (b d) -> p (a b) d", d=D)
        prod_junk = hid[:, 6:8, :].rearrange("p a h -> p (a h)")

        adj_in = [sem(f"adj_in{i}") for i in range(SLOTS)]
        x_in, w_in, weights_in = sem("x_in"), sem("w_in"), sem("weights_in")
        y_out = [sem(f"y_out{i}") for i in range(2)]
        ident_zero, ident_set, half_set = sem("ident_zero"), sem("ident_set"), sem("half_set")
        w_hi, w_lo, w2_scaled, beta_set = sem("w_hi"), sem("w_lo"), sem("w2_scaled"), sem("beta_set")
        bw_done, bw_set = sem("bw_done"), sem("bw_set")
        h_set, ht_done, ht_set = sem("h_set"), sem("ht_done"), sem("ht_set")
        x_hi, x_lo, resid_add, resid_set = sem("x_hi"), sem("x_lo"), sem("resid_add"), sem("resid_set")
        count_set, binv_set = sem("count_set"), sem("binv_set")
        dsum_set, dsafe_set, drec_set, dinv_set = sem("dsum_set"), sem("dsafe_set"), sem("drec_set"), sem("dinv_set")
        u_done, v_done, z_done, tT_done = sem("u_done"), sem("v_done"), sem("z_done"), sem("tT_done")
        q_done, p_done, s_done = sem("q_done"), sem("p_done"), sem("s_done")
        u_scaled, u_whole, u_hi, u_lo = sem("u_scaled"), sem("u_whole"), sem("u_hi"), sem("u_lo")
        p_scaled, p_whole, p_hi, p_lo = sem("p_scaled"), sem("p_whole"), sem("p_hi"), sem("p_lo")
        v_hi, v_lo = sem("v_hi"), sem("v_lo")
        z_set, relu_set, bn_set, mv_set = sem("z_set"), sem("relu_set"), sem("bn_set"), sem("mv_set")
        veps_set, rstd_set, t_set = sem("veps_set"), sem("rstd_set"), sem("t_set")
        tT_hi, tT_lo = sem("tT_hi"), sem("tT_lo")
        q_copied, q_beta, q_whole, q_hi, q_lo = (sem("q_copied"), sem("q_beta"), sem("q_whole"),
                                                 sem("q_hi"), sem("q_lo"))
        s_scaled, s_resid, s_set = sem("s_scaled"), sem("s_resid"), sem("s_set")
        bn2_set, mv2_set, veps2_set, rstd2_set, y_set = (sem("bn2_set"), sem("mv2_set"),
                                                         sem("veps2_set"), sem("rstd2_set"), sem("y_set"))

        def over_graphs(eng, body):
            body(0, True, False)
            with eng.Fori(1, N - 1) as n:
                body(n, False, False)
            body(N - 1, False, True)

        block = ctx.enter_context(nc.Block())

        @block.sync
        def _(sp):
            def load_adj(n, k):
                sp.dma_start(adj_sb[:, k % SLOTS, :], adj_rows[n, :, k, :]).then_inc(adj_in[k % SLOTS], 16)

            load_adj(0, 0)
            sp.dma_start(x_sb[:], x_rows[0]).then_inc(x_in, 16)
            for k in range(1, SLOTS):
                load_adj(0, k)
            for k in range(SLOTS, K):
                sp.wait_ge(h_set, k - SLOTS + 1)
                load_adj(0, k)

            def graph(n, first, last):
                if not last:
                    for k in range(SLOTS):
                        sp.wait_ge(h_set, n * K + K - SLOTS + k + 1)
                        load_adj(n + 1, k)
                    sp.wait_ge(resid_set, (n + 1) * K)
                    sp.wait_ge(x_lo, n + 1)
                    sp.dma_start(x_sb[:], x_rows[n + 1]).then_inc(x_in, 16)
                    sp.wait_ge(dsum_set, (n + 1) * K)
                    sp.dma_start(w_row[:], adj[n + 1, 0, :].partition_broadcast(P)).then_inc(w_in, 16)
                    for k in range(SLOTS, K):
                        sp.wait_ge(h_set, (n + 1) * K + k - SLOTS + 1)
                        load_adj(n + 1, k)
                for i in range(PAIRS):
                    sp.wait_ge(y_set, n * K + 2 * i + 2)
                    sp.dma_start(out_rows[n, :, 2 * i:2 * i + 2, :],
                                 y_sb[:, 2 * (i % 2):2 * (i % 2) + 2, :]).then_inc(y_out[i % 2], 16)

            over_graphs(sp, graph)
            for i in range(2):
                sp.wait_ge(y_out[i], 16 * N * PAIRS // 2)

        @block.scalar
        def _(act):
            act.dma_start(w1_raw, w1t.rearrange("(b p) h -> p b h", p=P)).then_inc(weights_in, 16)
            act.dma_start(w2_raw, w2t.rearrange("(b p) d -> p b d", p=P)).then_inc(weights_in, 16)
            act.dma_start(w_row[:], adj[0, 0, :].partition_broadcast(P)).then_inc(w_in, 16)
            act.dma_start(b1_row[:], b1.partition_broadcast(P)).then_inc(weights_in, 16)
            act.dma_start(b2_row[:], b2.partition_broadcast(P)).then_inc(weights_in, 16)
            act.dma_start(gcol[:], gamma).then_inc(weights_in, 16)
            act.dma_start(bcol[:], beta).then_inc(weights_in, 16)

            def split_x(n):
                act.wait_ge(x_in, 16 * (n + 1))
                nc.scalar.activation(feat[:, :, 0:D], x_sb[:], ACT.Copy).then_inc(x_hi, 1)

            split_x(0)
            act.wait_ge(weights_in, 96)
            nc.scalar.activation(w1p[:, 0], w1_raw, ACT.Copy).then_inc(w_hi, 1)
            act.wait_ge(w2_scaled, HB)
            nc.scalar.activation(w2p[:, :, 0:D], w2_raw, ACT.Copy).then_inc(w_hi, 1)

            def graph(n, first, last):
                def store_ht(j, half_):
                    act.wait_ge(ht_done, n * K * CH + j * CH + half_ + 1)
                    nc.scalar.activation(HT[:, j, half_ * BANK:(half_ + 1) * BANK], banks[4 + half_][:, :], ACT.Copy,
                                         accum_out=count[:, j, half_:half_ + 1]).then_inc(ht_set, 1)

                if not first:
                    act.wait_ge(s_done, n * K)
                for h in range(CH):
                    store_ht(0, h)
                for j in range(K):
                    act.wait_ge(u_done, n * K + j + 1)
                    act.wait_ge(binv_set, n * K + j + 1)
                    if j >= 2:
                        act.wait_ge(u_whole, n * K + j - 1)
                    elif not first:
                        act.wait_ge(s_resid, n * K)
                    nc.scalar.activation(scaled_lo[:, j % 2, :], banks[6 + j % 2][:, D:2 * D], ACT.Copy,
                                         scale=binv[:, j:j + 1]).then_inc(u_scaled, 1)
                    if j + 1 < K:
                        store_ht(j + 1, 0)
                    act.wait_ge(u_whole, n * K + j + 1)
                    nc.scalar.activation(mid[:, j, 0:D], whole[:, j % 2, :], ACT.Copy).then_inc(u_hi, 1)
                    if j + 1 < K:
                        store_ht(j + 1, 1)
                for g in range(DB * CH):
                    h, b = g // DB, g % DB
                    act.wait_ge(v_done, n * DB * CH + g + 1)
                    nc.scalar.activation(vT[:, 0, b, h * BANK:(h + 1) * BANK], banks[g][:, :],
                                         ACT.Copy).then_inc(v_hi, 1)
                for j in range(K):
                    act.wait_ge(z_set, n * K + j + 1)
                    nc.scalar.activation(hid[:, j, :], hid[:, j, :], ACT.Relu).then_inc(relu_set, 1)

                def store_tT(j):
                    act.wait_ge(tT_done, n * K + j + 1)
                    if j >= 2:
                        act.wait_ge(q_done, n * K + j - 1)
                    nc.scalar.activation(hidT[:, j % 2, 0].rearrange("p b m -> p (b m)"), banks[j % 2][:, :],
                                         ACT.Copy).then_inc(tT_hi, 1)

                store_tT(0)
                for j in range(K):
                    if j + 1 < K:
                        store_tT(j + 1)
                    act.wait_ge(q_done, n * K + j + 1)
                    if j >= 2:
                        act.wait_ge(q_beta, n * K + j - 1)
                    nc.scalar.activation(scaled_lo[:, j % 2, :], banks[2 + j % 2][:, D:2 * D],
                                         ACT.Copy).then_inc(q_copied, 1)
                    act.wait_ge(q_whole, n * K + j + 1)
                    nc.scalar.activation(feat[:, j, 0:D], whole[:, j % 2, :], ACT.Copy).then_inc(q_hi, 1)
                for j in range(K):
                    act.wait_ge(p_done, n * K + j + 1)
                    if j < 2:
                        act.wait_ge(q_beta, n * K + K)
                    else:
                        act.wait_ge(p_whole, n * K + j - 1)
                    nc.scalar.activation(scaled_lo[:, j % 2, :], banks[4 + j % 4][:, D:2 * D], ACT.Copy,
                                         scale=binv[:, j:j + 1]).then_inc(p_scaled, 1)
                    act.wait_ge(p_whole, n * K + j + 1)
                    nc.scalar.activation(mid[:, j, 0:D], whole[:, j % 2, :], ACT.Copy).then_inc(p_hi, 1)
                for j in range(K):
                    act.wait_ge(s_done, n * K + j + 1)
                    if j < 2:
                        act.wait_ge(p_whole, n * K + K)
                    else:
                        act.wait_ge(s_resid, n * K + j - 1)
                    nc.scalar.activation(scaled_lo[:, j % 2, :], banks[j % 4][:, D:2 * D], ACT.Copy,
                                         scale=dinv[:, j:j + 1]).then_inc(s_scaled, 1)
                    if j == 0 and not last:
                        split_x(n + 1)

            over_graphs(act, graph)

        @block.gpsimd
        def _(pool):
            nc.gpsimd.memset(ident[:], 0.0).then_inc(ident_zero, 1)
            nc.gpsimd.memset(half[:], -0.5).then_inc(half_set, 1)
            pool.wait_ge(ident_zero, 1)
            nc.gpsimd.affine_select(out=ident[:], in_=ident[:], compare_op=ALU.not_equal, fill=1.0, base=0,
                                    pattern=[[-1, P]], channel_multiplier=1).then_inc(ident_set, 1)
            pool.wait_ge(half_set, 1)

            def split_x(n):
                pool.wait_ge(x_hi, n + 1)
                nc.gpsimd.tensor_tensor(feat[:, :, D:2 * D], x_sb[:], feat[:, :, 0:D].bitcast(F32),
                                        ALU.subtract).then_inc(x_lo, 1)

            split_x(0)
            pool.wait_ge(w_hi, 2)
            pool.wait_ge(w_lo, 2)
            pool.wait_ge(bw_done, 1)

            def graph(n, first, last):
                if not first:
                    pool.wait_ge(s_resid, n * K)
                pool.wait_ge(x_in, 16 * (n + 1))
                for j in range(K):
                    nc.gpsimd.tensor_tensor(resid[:, j, :], x_sb[:, j, :], b2_row[:], ALU.add).then_inc(resid_add, 1)
                    pool.wait_ge(resid_add, n * K + j + 1)
                    nc.gpsimd.tensor_tensor(resid[:, j, :], resid[:, j, :], x_sb[:, j, :],
                                            ALU.add).then_inc(resid_set, 1)
                for j in range(K):
                    pool.wait_ge(u_hi, n * K + j + 1)
                    nc.gpsimd.tensor_tensor(mid[:, j, D:2 * D], whole[:, j % 2, :], mid[:, j, 0:D].bitcast(F32),
                                            ALU.subtract).then_inc(u_lo, 1)
                for i in range(PAIRS):
                    pool.wait_ge(veps_set, n * PAIRS + i + 1)
                    nc.gpsimd.tensor_tensor(rstd[:, 2 * i:2 * i + 2], veps[:, 2 * i:2 * i + 2], half[:],
                                            ALU.pow).then_inc(rstd_set, 1)
                for j in range(K):
                    pool.wait_ge(q_copied, n * K + j + 1)
                    if j >= 2:
                        pool.wait_ge(q_whole, n * K + j - 1)
                    elif not first:
                        pool.wait_ge(s_set, n * K)
                    nc.gpsimd.tensor_tensor(add_lo[:, j % 2, :], scaled_lo[:, j % 2, :], bw_row[:],
                                            ALU.add).then_inc(q_beta, 1)
                    pool.wait_ge(q_hi, n * K + j + 1)
                    nc.gpsimd.tensor_tensor(feat[:, j, D:2 * D], whole[:, j % 2, :], feat[:, j, 0:D].bitcast(F32),
                                            ALU.subtract).then_inc(q_lo, 1)
                for j in range(K):
                    pool.wait_ge(p_hi, n * K + j + 1)
                    nc.gpsimd.tensor_tensor(mid[:, j, D:2 * D], whole[:, j % 2, :], mid[:, j, 0:D].bitcast(F32),
                                            ALU.subtract).then_inc(p_lo, 1)
                for j in range(K):
                    pool.wait_ge(s_scaled, n * K + j + 1)
                    if j < 2:
                        pool.wait_ge(q_whole, n * K + K)
                    else:
                        pool.wait_ge(s_set, n * K + j - 1)
                    nc.gpsimd.tensor_tensor(add_lo[:, j % 2, :], scaled_lo[:, j % 2, :], resid[:, j, :],
                                            ALU.add).then_inc(s_resid, 1)
                    if j % 2 and j >= 3:
                        norm_power(n, j // 2 - 1)
                    if j == 2 and not last:
                        split_x(n + 1)
                norm_power(n, PAIRS - 1)

            def norm_power(n, i):
                pool.wait_ge(veps2_set, n * PAIRS + i + 1)
                nc.gpsimd.tensor_tensor(rstd2[:, 2 * i:2 * i + 2], veps2[:, 2 * i:2 * i + 2], half[:],
                                        ALU.pow).then_inc(rstd2_set, 1)

            over_graphs(pool, graph)

        @block.vector
        def _(dve):
            def set_h(n, k):
                dve.wait_ge(adj_in[k % SLOTS], 16 * (2 * n + k // SLOTS + 1))
                nc.vector.tensor_scalar(H[:, k, :], adj_sb[:, k % SLOTS, :], 0.0, None,
                                        ALU.not_equal).then_inc(h_set, 1)

            for k in range(SLOTS):
                set_h(0, k)
            dve.wait_ge(weights_in, 96)
            for b in range(HB):
                nc.vector.tensor_copy(beta_cols[:, b, :], bcol[:, b:b + 1].to_broadcast([P, P])).then_inc(beta_set, 1)
            dve.wait_ge(w_hi, 1)
            nc.vector.tensor_tensor(w1p[:, 1], w1_raw, w1p[:, 0].bitcast(F32), ALU.subtract).then_inc(w_lo, 1)
            for k in range(SLOTS, K):
                set_h(0, k)
            dve.wait_ge(bw_done, 1)
            nc.vector.tensor_copy(bw_row[:], banks[0][:, 0:D]).then_inc(bw_set, 1)
            for b in range(HB):
                nc.vector.tensor_scalar(w2_raw[:, b, :], w2_raw[:, b, :], gcol[:, b:b + 1], None,
                                        ALU.mult).then_inc(w2_scaled, 1)
            dve.wait_ge(w2_scaled, HB)
            dve.wait_ge(w_hi, 2)
            nc.vector.tensor_tensor(w2p[:, :, D:2 * D], w2_raw, w2p[:, :, 0:D].bitcast(F32),
                                    ALU.subtract).then_inc(w_lo, 1)

            def graph(n, first, last):
                def column_inverse(j):
                    dve.wait_ge(ht_set, n * K * CH + (j + 1) * CH)
                    nc.vector.tensor_scalar(count1[:, j:j + 1], count[:, j, 0:1], count[:, j, 1:2], 1.0,
                                            ALU.add, ALU.max).then_inc(count_set, 1)
                    dve.wait_ge(count_set, n * K + j + 1)
                    nc.vector.reciprocal(binv[:, j:j + 1], count1[:, j:j + 1]).then_inc(binv_set, 1)

                def combine(j, scaled, lo_done, done, bank):
                    dve.wait_ge(scaled, n * K + j + 1)
                    if j >= 2:
                        dve.wait_ge(lo_done, n * K + j - 1)
                    nc.vector.scalar_tensor_tensor(whole[:, j % 2, :], bank[:, 0:D], binv[:, j:j + 1],
                                                   scaled_lo[:, j % 2, :], ALU.mult, ALU.add).then_inc(done, 1)

                if not first:
                    dve.wait_ge(tT_done, n * K)
                    dve.wait_ge(y_set, n * K)
                column_inverse(0)
                dve.wait_ge(w_in, 16 * (n + 1))
                for j in range(K):
                    if j > 0:
                        column_inverse(j)
                    if j == 0 and not first:
                        dve.wait_ge(p_lo, n * K)
                    combine(j, u_scaled, u_lo, u_whole, banks[6 + j % 2])
                    dve.wait_ge(h_set, n * K + j + 1)
                    if first and j == 0:
                        pass
                    elif j > 0:
                        dve.wait_ge(dsum_set, n * K + j)
                    nc.vector.tensor_tensor_reduce(out=prod_junk, in0=H[:, j, :].bitcast(F32), in1=w_row[:],
                                                   scale=1.0, scalar=0.0, op0=ALU.mult, op1=ALU.add,
                                                   accum_out=dsum[:, j:j + 1]).then_inc(dsum_set, 1)
                dve.wait_ge(dsum_set, (n + 1) * K)
                nc.vector.scalar_tensor_tensor(dsafe[:], dsum[:], 0.0, dsum[:], ALU.is_le,
                                               ALU.max).then_inc(dsafe_set, 1)
                dve.wait_ge(dsafe_set, n + 1)
                nc.vector.reciprocal(drec[:], dsafe[:]).then_inc(drec_set, 1)
                dve.wait_ge(drec_set, n + 1)
                nc.vector.scalar_tensor_tensor(dinv[:], dsum[:], 0.0, drec[:], ALU.is_gt,
                                               ALU.mult).then_inc(dinv_set, 1)
                dve.wait_ge(dinv_set, n + 1)
                for g in range(DB * CH):
                    h, b = g // DB, g % DB
                    dve.wait_ge(v_hi, n * DB * CH + g + 1)
                    nc.vector.tensor_tensor(vT[:, 1, b, h * BANK:(h + 1) * BANK], banks[g][:, :],
                                            vT[:, 0, b, h * BANK:(h + 1) * BANK].bitcast(F32),
                                            ALU.subtract).then_inc(v_lo, 1)

                def normalize(i):
                    dve.wait_ge(rstd_set, n * PAIRS + i + 1)
                    for j in (2 * i, 2 * i + 1):
                        nc.vector.tensor_scalar(hid[:, j, :], hid[:, j, :], mv[:, j, 0:1], rstd[:, j:j + 1],
                                                ALU.subtract, ALU.mult).then_inc(t_set, 1)

                def aggregate(j):
                    nc.vector.bn_aggr(mv[:, j, :], stats[:, j, :]).then_inc(mv_set, 1)
                    if j % 2:
                        dve.wait_ge(mv_set, n * K + j + 1)
                        nc.vector.tensor_scalar(veps[:, j - 1:j + 1], mv[:, j - 1:j + 1, 1], EPS, None,
                                                ALU.add).then_inc(veps_set, 1)

                for j in range(K + 1):
                    if j < K:
                        dve.wait_ge(z_done, n * K + j + 1)
                        nc.vector.scalar_tensor_tensor(hid[:, j, :], banks[4 + j % 4][:, :], dinv[:, j:j + 1],
                                                       b1_row[:], ALU.mult, ALU.add).then_inc(z_set, 1)
                    if j > 0:
                        if j > 1:
                            dve.wait_ge(bn_set, n * K + j - 1)
                        dve.wait_ge(relu_set, n * K + j)
                        nc.vector.bn_stats(stats[:, j - 1, :], hid[:, j - 1, :]).then_inc(bn_set, 1)
                    if j > 1:
                        aggregate(j - 2)
                    if j > 3 and j % 2:
                        normalize((j - 5) // 2)
                dve.wait_ge(bn_set, n * K + K)
                normalize(PAIRS - 2)
                aggregate(K - 1)
                normalize(PAIRS - 1)

                def rest_of_tT(j):
                    dve.wait_ge(tT_hi, n * K + j + 1)
                    nc.vector.tensor_tensor(hidT[:, j % 2, 1].rearrange("p b m -> p (b m)"), banks[j % 2][:, :],
                                            hidT[:, j % 2, 0].rearrange("p b m -> p (b m)").bitcast(F32),
                                            ALU.subtract).then_inc(tT_lo, 1)

                rest_of_tT(0)
                for j in range(K):
                    if j + 1 < K:
                        rest_of_tT(j + 1)
                    dve.wait_ge(q_beta, n * K + j + 1)
                    if j < 2:
                        dve.wait_ge(u_lo, n * K + K)
                    else:
                        dve.wait_ge(q_lo, n * K + j - 1)
                    nc.vector.tensor_tensor(whole[:, j % 2, :], banks[2 + j % 2][:, 0:D], add_lo[:, j % 2, :],
                                            ALU.add).then_inc(q_whole, 1)
                dve.wait_ge(q_lo, n * K + K)
                for j in range(K):
                    combine(j, p_scaled, p_lo, p_whole, banks[4 + j % 4])

                def finish(i):
                    dve.wait_ge(rstd2_set, n * PAIRS + i + 1)
                    if i >= 2 or not first:
                        dve.wait_ge(y_out[i % 2], 16 * (n * (PAIRS // 2) + i // 2))
                    for j in (2 * i, 2 * i + 1):
                        nc.vector.tensor_scalar(y_sb[:, j % 4, :], ssum[:, j, :], mv2[:, j, 0:1],
                                                rstd2[:, j:j + 1], ALU.subtract, ALU.mult).then_inc(y_set, 1)

                def aggregate2(j):
                    nc.vector.bn_aggr(mv2[:, j, :], stats2[:, j, :]).then_inc(mv2_set, 1)
                    if j % 2:
                        dve.wait_ge(mv2_set, n * K + j + 1)
                        nc.vector.tensor_scalar(veps2[:, j - 1:j + 1], mv2[:, j - 1:j + 1, 1], EPS, None,
                                                ALU.add).then_inc(veps2_set, 1)

                if not last:
                    dve.wait_ge(p_done, n * K + K)
                    set_h(n + 1, 0)
                    set_h(n + 1, 1)
                for j in range(K):
                    dve.wait_ge(s_resid, n * K + j + 1)
                    nc.vector.scalar_tensor_tensor(ssum[:, j, :], banks[j % 4][:, 0:D], dinv[:, j:j + 1],
                                                   add_lo[:, j % 2, :], ALU.mult, ALU.add).then_inc(s_set, 1)
                    if not last and j + 2 < K:
                        set_h(n + 1, j + 2)
                    if j > 0:
                        dve.wait_ge(bn2_set, n * K + j)
                    dve.wait_ge(s_set, n * K + j + 1)
                    nc.vector.bn_stats(stats2[:, j, :], ssum[:, j, :]).then_inc(bn2_set, 1)
                    if j > 0:
                        aggregate2(j - 1)
                    if j > 3 and j % 2 == 0:
                        finish(j // 2 - 2)
                dve.wait_ge(bn2_set, n * K + K)
                finish(PAIRS - 2)
                aggregate2(K - 1)
                finish(PAIRS - 1)

            over_graphs(dve, graph)

        @block.tensor
        def _(pe):
            pe.wait_ge(beta_set, HB)
            pe.wait_ge(weights_in, 96)
            for b in range(HB):
                last_mm = nc.tensor.matmul(banks[0][:, 0:D], beta_cols[:, b, :], w2_raw[:, b, :],
                                           start=(b == 0), stop=(b == HB - 1))
            last_mm.then_inc(bw_done, 1)
            pe.wait_ge(ident_set, 1)
            Hf = H[:].bitcast(F32)

            def graph(n, first, last):
                def transpose_h(j):
                    for k in range(K):
                        if j == 0:
                            pe.wait_ge(h_set, n * K + k + 1)
                        if k % 4 == 0:
                            if j > 0:
                                pe.wait_ge(ht_set, n * K * CH + (j - 1) * CH + k // 4 + 1)
                            elif not first:
                                pe.wait_ge(p_whole, n * K)
                        mm = nc.tensor.transpose(banks[4 + k // 4][:, (k % 4) * P:(k % 4 + 1) * P],
                                                 Hf[:, k, j * P:(j + 1) * P], ident[:])
                        if k % 4 == 3:
                            mm.then_inc(ht_done, 1)

                transpose_h(0)
                pe.wait_ge(x_lo, n + 1)
                for j in range(K):
                    if j >= 2:
                        pe.wait_ge(u_whole, n * K + j - 1)
                    for k in range(K):
                        mm = nc.tensor.matmul(banks[6 + j % 2][:, :], H[:, k, j * P:(j + 1) * P], feat[:, k, :],
                                              start=(k == 0), stop=(k == K - 1))
                    mm.then_inc(u_done, 1)
                    if j + 1 < K:
                        transpose_h(j + 1)
                if not first:
                    pe.wait_ge(s_set, n * K)
                else:
                    pe.wait_ge(bw_set, 1)
                for g in range(DB * CH):
                    h, b = g // DB, g % DB
                    for k in range(K):
                        for part in range(2):
                            if g == 0:
                                pe.wait_ge((u_hi, u_lo)[part], n * K + k + 1)
                                pe.wait_ge(ht_set, n * K * CH + (k + 1) * CH)
                            mm = nc.tensor.matmul(banks[g][:, :], mid[:, k, part * D + b * P:part * D + (b + 1) * P],
                                                  HT[:, k, h * BANK:(h + 1) * BANK],
                                                  start=(k == 0 and part == 0), stop=(k == K - 1 and part == 1))
                    mm.then_inc(v_done, 1)
                if first:
                    pe.wait_ge(w_lo, 2)
                for j in range(K):
                    if j % 4 == 0:
                        pe.wait_ge(v_lo, n * DB * CH + (j // 4 + 1) * DB)
                    if j >= 4:
                        pe.wait_ge(z_set, n * K + j - 3)
                    for b in range(DB):
                        for part in range(2):
                            for wpart in range(2):
                                mm = nc.tensor.matmul(banks[4 + j % 4][:, :], vT[:, part, b, j * P:(j + 1) * P],
                                                      w1p[:, wpart, b, :], start=(b + part + wpart == 0),
                                                      stop=(b + part + wpart == DB + 1))
                    mm.then_inc(z_done, 1)

                def transpose_t(j):
                    pe.wait_ge(t_set, n * K + j + 1)
                    if j >= 2:
                        pe.wait_ge(tT_lo, n * K + j - 1)
                    for b in range(HB):
                        mm = nc.tensor.transpose(banks[j % 2][:, b * P:(b + 1) * P], hid[:, j, b * P:(b + 1) * P],
                                                 ident[:])
                    mm.then_inc(tT_done, 1)

                transpose_t(0)
                for j in range(K):
                    if j + 1 < K:
                        transpose_t(j + 1)
                    pe.wait_ge(tT_lo, n * K + j + 1)
                    if j >= 2:
                        pe.wait_ge(q_whole, n * K + j - 1)
                    for b in range(HB):
                        for part in range(2):
                            mm = nc.tensor.matmul(banks[2 + j % 2][:, :], hidT[:, j % 2, part, b, :], w2p[:, b, :],
                                                  start=(b + part == 0), stop=(b + part == HB))
                    mm.then_inc(q_done, 1)
                for j in range(0, K, 2):
                    for k in range(K):
                        if j == 0:
                            pe.wait_ge(q_lo, n * K + k + 1)
                        for jj in (j, j + 1):
                            if k == 0 and jj >= 4:
                                pe.wait_ge(p_whole, n * K + jj - 3)
                            mm = nc.tensor.matmul(banks[4 + jj % 4][:, :], H[:, k, jj * P:(jj + 1) * P],
                                                  feat[:, k, :], start=(k == 0), stop=(k == K - 1))
                            if k == K - 1:
                                mm.then_inc(p_done, 1)
                for j in range(0, K, 2):
                    for k in range(K):
                        if j == 0:
                            pe.wait_ge(p_lo, n * K + k + 1)
                        for jj in (j, j + 1):
                            if k == 0 and jj >= 4:
                                pe.wait_ge(s_set, n * K + jj - 3)
                            mm = nc.tensor.matmul(banks[jj % 4][:, :], HT[:, k, jj * P:(jj + 1) * P],
                                                  mid[:, k, :], start=(k == 0), stop=(k == K - 1))
                            if k == K - 1:
                                mm.then_inc(s_done, 1)

            over_graphs(pe, graph)


def kernel(**inputs):
    import numpy as np
    import concourse.bacc as bacc
    from concourse.bass_utils import run_bass_kernel_spmd

    laid_out = {
        "x": inputs["x"], "adj": inputs["adj"],
        "w1t": np.asarray(inputs["L0_gnn_W1"]).T, "b1": inputs["L0_gnn_b1"],
        "gamma": np.asarray(inputs["L0_gnn_gamma"]).reshape(-1, P).T, "beta": np.asarray(inputs["L0_gnn_beta"]).reshape(-1, P).T,
        "w2t": np.asarray(inputs["L0_gnn_W2"]).T, "b2": inputs["L0_gnn_b2"],
    }
    nc = bacc.Bacc("TRN2", target_bir_lowering=False, num_devices=1)
    arrays, args = {}, []
    for name, value in laid_out.items():
        a = np.ascontiguousarray(value)
        arrays[f"in_{name}"] = a
        args.append(nc.dram_tensor(f"in_{name}", a.shape, mybir.dt.from_np(a.dtype), kind="ExternalInput").ap())
    shape = arrays["in_x"].shape
    args.append(nc.dram_tensor("out_0", shape, F32, kind="ExternalOutput").ap())
    graph_kernel(nc, *args)
    result = run_bass_kernel_spmd(nc, [arrays], core_ids=[0])
    return result.results[0]["out_0"]
```

```python
from contextlib import ExitStack

import concourse.bass as bass
from concourse import mybir

P = 128
F32 = mybir.dt.float32
F32R = mybir.dt.float32r
BF16 = mybir.dt.bfloat16
ALU = mybir.AluOpType
ACT = mybir.ActivationFunctionType
EPS = 1e-5
SLOTS = 4
BANK = 512
T_LAG = 5
Q_LAG = 6


def graph_kernel(nc: bass.Bass, x, adj, w1t, b1, gamma, beta, w2t, b2, out):
    N, C, D = x.shape
    DH = w1t.shape[1]
    K = C // P
    DB = D // P
    HB = DH // P
    CH = C // BANK
    PAIRS = K // 2
    assert C == K * P and D * 2 == BANK and DH == BANK and K == 8 and SLOTS * 2 == K and N >= 3

    adj_rows = adj.rearrange("n (p k) e -> n p k e", k=K)
    x_rows = x.rearrange("n (p k) d -> n p k d", k=K)
    out_rows = out.rearrange("n (p k) d -> n p k d", k=K)

    with ExitStack() as ctx:
        def sb(name, shape, dt=F32):
            return ctx.enter_context(nc.sbuf_tensor(name, shape, dt))

        def sem(name):
            return ctx.enter_context(nc.semaphore(name))

        adj_sb = sb("adj_sb", [P, SLOTS, C])
        H = sb("H", [P, K, C], F32R)
        HT = sb("HT", [P, K, C], F32R)
        x_sb = sb("x_sb", [P, K, D])
        resid = sb("resid", [P, K, D])
        feat = sb("feat", [P, K, 2 * D], F32R)
        mid = sb("mid", [P, K, 2 * D], F32R)
        shared = nc.sbuf_base
        vT = sb("vT", [P, 2, DB, C], F32R)
        H16 = nc.alloc_sbuf_tensor_at("H16", [P, K, C], BF16, offset=shared)
        hid = sb("hid", [P, K, DH])
        hidT = sb("hidT", [P, 2, 2, HB, P], F32R)
        w1p = sb("w1p", [P, 2, DB, DH], F32R)
        w2p = sb("w2p", [P, HB, 2 * D], F32R)
        w_row = sb("w_row", [P, C])
        b1_row = sb("b1_row", [P, DH])
        b2_row = sb("b2_row", [P, D])
        bw_row = sb("bw_row", [P, D])
        ident = sb("ident", [P, P])
        ident16 = sb("ident16", [P, P], BF16)
        scaled_lo = sb("scaled_lo", [P, 2, D])
        add_lo = sb("add_lo", [P, 2, D])
        whole = sb("whole", [P, 2, D])
        gcol = sb("gcol", [P, HB])
        bcol = sb("bcol", [P, HB])
        half = sb("half", [P, K])
        count = sb("count", [P, K])
        count1 = sb("count1", [P, K])
        binv = sb("binv", [P, K])
        dsum = sb("dsum", [P, K])
        dsafe = sb("dsafe", [P, K])
        drec = sb("drec", [P, K])
        dinv = sb("dinv", [P, K])
        stats = sb("stats", [P, K, 6])
        mv = sb("mv", [P, K, 2])
        veps = sb("veps", [P, K])
        rstd = sb("rstd", [P, K])
        stats2 = sb("stats2", [P, K, 6])
        mv2 = sb("mv2", [P, K, 2])
        veps2 = sb("veps2", [P, K])
        rstd2 = sb("rstd2", [P, K])
        banks = [ctx.enter_context(nc.psum_tensor(f"bank{i}", [P, BANK], F32)) for i in range(8)]

        w1_raw = resid[:, 0:4, :].rearrange("p a d -> p (a d)").rearrange("p (b h) -> p b h", b=DB)
        w2_raw = resid[:, 4:8, :]
        beta_cols = hid[:, 0, :].rearrange("p (b m) -> p b m", b=HB)
        ssum = hid[:, 0:K // 2, :].rearrange("p a (b d) -> p (a b) d", d=D)
        prod_junk = hid[:, 6:8, :].rearrange("p a h -> p (a h)")

        adj_in = [sem(f"adj_in{i}") for i in range(SLOTS)]
        x_in, w_in, weights_in = sem("x_in"), sem("w_in"), sem("weights_in")
        y_out = [sem(f"y_out{i}") for i in range(PAIRS)]
        ident_zero, ident_set, half_set = sem("ident_zero"), sem("ident_set"), sem("half_set")
        w_hi, w_lo, w2_scaled, beta_set = sem("w_hi"), sem("w_lo"), sem("w2_scaled"), sem("beta_set")
        bw_done, bw_set = sem("bw_done"), sem("bw_set")
        h16_set, h_even, h_odd = sem("h16_set"), sem("h_even"), sem("h_odd")
        ht_done, ht_set = sem("ht_done"), sem("ht_set")
        x_hi, x_lo, resid_set = sem("x_hi"), sem("x_lo"), sem("resid_set")
        count_set, binv_set = sem("count_set"), sem("binv_set")
        dsum_set, dsafe_set, drec_set, dinv_set = sem("dsum_set"), sem("dsafe_set"), sem("drec_set"), sem("dinv_set")
        u_done, v_done, z_done, tT_done = sem("u_done"), sem("v_done"), sem("z_done"), sem("tT_done")
        q_done, p_done, s_done = sem("q_done"), sem("p_done"), sem("s_done")
        u_scaled, u_whole, u_hi, u_lo = sem("u_scaled"), sem("u_whole"), sem("u_hi"), sem("u_lo")
        p_scaled, p_whole, p_hi, p_lo = sem("p_scaled"), sem("p_whole"), sem("p_hi"), sem("p_lo")
        v_hi, v_lo = sem("v_hi"), sem("v_lo")
        z_set, relu_set, bn_set, mv_set = sem("z_set"), sem("relu_set"), sem("bn_set"), sem("mv_set")
        veps_set, rstd_set, t_set = sem("veps_set"), sem("rstd_set"), sem("t_set")
        tT_hi, tT_lo = sem("tT_hi"), sem("tT_lo")
        q_copied, q_beta, q_whole, q_hi, q_lo = (sem("q_copied"), sem("q_beta"), sem("q_whole"),
                                                 sem("q_hi"), sem("q_lo"))
        s_scaled, s_resid, s_set = sem("s_scaled"), sem("s_resid"), sem("s_set")
        bn2_set, mv2_set, veps2_set, rstd2_set, y_set = (sem("bn2_set"), sem("mv2_set"),
                                                         sem("veps2_set"), sem("rstd2_set"), sem("y_set"))

        EARLY = K - 2
        P_ORDER = ([(j, range(EARLY)) for j in range(4)] + [(j, range(EARLY, K)) for j in range(4)]
                   + [(j, range(K)) for j in range(4, K)])

        def over_graphs(eng, body):
            body(0, True, False)
            with eng.Fori(0, N - 2) as m:
                body(m + 1, False, False)
            body(N - 1, False, True)

        block = ctx.enter_context(nc.Block())

        @block.sync
        def _(sp):
            def load_adj(n, k):
                sp.dma_start(adj_sb[:, k % SLOTS, :], adj_rows[n, :, k, :]).then_inc(adj_in[k % SLOTS], 16)

            def store_result(n):
                for i in range(PAIRS):
                    sp.wait_ge(y_set, n * K + 2 * i + 2)
                    sp.dma_start(out_rows[n, :, 2 * i:2 * i + 2, :],
                                 ssum[:, 2 * i:2 * i + 2, :]).then_inc(y_out[i], 16)

            for k in range(SLOTS):
                load_adj(0, k)
            sp.dma_start(x_sb[:], x_rows[0]).then_inc(x_in, 16)
            for k in range(SLOTS, K):
                sp.wait_ge(h16_set, k - SLOTS + 1)
                load_adj(0, k)

            def graph(n, first, last):
                if not last:
                    for k in range(SLOTS):
                        sp.wait_ge(h16_set, n * K + K - SLOTS + k + 1)
                        load_adj(n + 1, k)
                    sp.wait_ge(dsum_set, (n + 1) * K)
                    sp.dma_start(w_row[:], adj[n + 1, 0, :].partition_broadcast(P)).then_inc(w_in, 16)
                if not first:
                    store_result(n - 1)
                if not last:
                    for k in range(SLOTS, K):
                        sp.wait_ge(h16_set, (n + 1) * K + k - SLOTS + 1)
                        load_adj(n + 1, k)
                        if k == SLOTS + 1:
                            sp.wait_ge(resid_set, 2 * (n + 1))
                            sp.dma_start(x_sb[:], x_rows[n + 1]).then_inc(x_in, 16)
                else:
                    store_result(n)

            over_graphs(sp, graph)
            for i in range(PAIRS):
                sp.wait_ge(y_out[i], 16 * N)

        @block.scalar
        def _(act):
            act.dma_start(w1_raw, w1t.rearrange("(b p) h -> p b h", p=P)).then_inc(weights_in, 16)
            act.dma_start(w2_raw, w2t.rearrange("(b p) d -> p b d", p=P)).then_inc(weights_in, 16)
            act.dma_start(w_row[:], adj[0, 0, :].partition_broadcast(P)).then_inc(w_in, 16)
            act.dma_start(b1_row[:], b1.partition_broadcast(P)).then_inc(weights_in, 16)
            act.dma_start(b2_row[:], b2.partition_broadcast(P)).then_inc(weights_in, 16)
            act.dma_start(gcol[:], gamma).then_inc(weights_in, 16)
            act.dma_start(bcol[:], beta).then_inc(weights_in, 16)

            def odd_h(n, k):
                act.wait_ge(h16_set, n * K + k + 1)
                nc.scalar.activation(H[:, k, :], H16[:, k, :], ACT.Copy).then_inc(h_odd, 1)

            def x_high(n, i):
                if i == 0:
                    act.wait_ge(x_in, 16 * (n + 1))
                nc.scalar.activation(feat[:, 2 * i:2 * i + 2, 0:D], x_sb[:, 2 * i:2 * i + 2, :],
                                     ACT.Copy).then_inc(x_hi, 1)

            for k in (1, 3):
                odd_h(0, k)
            for i in range(PAIRS):
                x_high(0, i)
            for k in (5, 7):
                odd_h(0, k)
            act.wait_ge(weights_in, 96)
            nc.scalar.activation(w1p[:, 0], w1_raw, ACT.Copy).then_inc(w_hi, 1)

            def graph(n, first, last):
                def store_ht(j):
                    act.wait_ge(ht_done, n * K + j + 1)
                    nc.scalar.activation(HT[:, j, :], banks[4 + j % 2][:, :].bitcast(BF16), ACT.Copy,
                                         accum_out=count[:, j:j + 1]).then_inc(ht_set, 1)

                if not first:
                    act.wait_ge(s_done, n * K)
                    act.wait_ge(binv_set, n * K)
                store_ht(0)
                store_ht(1)
                for j in range(K):
                    act.wait_ge(u_done, n * K + j + 1)
                    act.wait_ge(binv_set, n * K + j + 1)
                    if j >= 2:
                        act.wait_ge(u_whole, n * K + j - 1)
                    elif not first:
                        act.wait_ge(s_resid, n * K)
                    nc.scalar.activation(scaled_lo[:, j % 2, :], banks[6 + j % 2][:, D:2 * D], ACT.Copy,
                                         scale=binv[:, j:j + 1]).then_inc(u_scaled, 1)
                    act.wait_ge(u_whole, n * K + j + 1)
                    nc.scalar.activation(mid[:, j, 0:D], whole[:, j % 2, :], ACT.Copy).then_inc(u_hi, 1)
                    if j + 2 < K:
                        store_ht(j + 2)
                if first:
                    act.wait_ge(w2_scaled, HB)
                    nc.scalar.activation(w2p[:, :, 0:D], w2_raw, ACT.Copy).then_inc(w_hi, 1)
                for g in range(DB * CH):
                    h, b = g // DB, g % DB
                    act.wait_ge(v_done, n * DB * CH + g + 1)
                    nc.scalar.activation(vT[:, 0, b, h * BANK:(h + 1) * BANK], banks[g][:, :],
                                         ACT.Copy).then_inc(v_hi, 1)
                for step in range(K + Q_LAG + 1):
                    j = step - Q_LAG - 1
                    if 0 <= j:
                        act.wait_ge(q_done, n * K + j + 1)
                        if j >= 2:
                            act.wait_ge(q_beta, n * K + j - 1)
                        nc.scalar.activation(scaled_lo[:, j % 2, :], banks[2 + j % 2][:, D:2 * D],
                                             ACT.Copy).then_inc(q_copied, 1)
                    if step < K:
                        act.wait_ge(z_set, n * K + step + 1)
                        nc.scalar.activation(hid[:, step, :], hid[:, step, :], ACT.Relu).then_inc(relu_set, 1)
                    i = step - T_LAG
                    if 0 <= i < K:
                        act.wait_ge(tT_done, n * K + i + 1)
                        if i >= 2:
                            act.wait_ge(q_done, n * K + i - 1)
                        nc.scalar.activation(hidT[:, i % 2, 0].rearrange("p b m -> p (b m)"), banks[i % 2][:, :],
                                             ACT.Copy).then_inc(tT_hi, 1)
                    if 0 <= j:
                        act.wait_ge(q_whole, n * K + j + 1)
                        nc.scalar.activation(feat[:, j, 0:D], whole[:, j % 2, :], ACT.Copy).then_inc(q_hi, 1)
                for j in range(K):
                    act.wait_ge(p_done, n * K + j + 1)
                    if j < 2:
                        act.wait_ge(q_beta, n * K + K)
                    else:
                        act.wait_ge(p_whole, n * K + j - 1)
                    nc.scalar.activation(scaled_lo[:, j % 2, :], banks[(4 + j) % 8][:, D:2 * D], ACT.Copy,
                                         scale=binv[:, j:j + 1]).then_inc(p_scaled, 1)
                    act.wait_ge(p_whole, n * K + j + 1)
                    nc.scalar.activation(mid[:, j, 0:D], whole[:, j % 2, :], ACT.Copy).then_inc(p_hi, 1)
                if not last:
                    odd_h(n + 1, 1)
                    odd_h(n + 1, 3)
                    odd_h(n + 1, 5)
                for j in range(K):
                    act.wait_ge(s_done, n * K + j + 1)
                    if j < 2:
                        act.wait_ge(p_whole, n * K + K)
                    else:
                        act.wait_ge(s_resid, n * K + j - 1)
                    nc.scalar.activation(scaled_lo[:, j % 2, :], banks[j][:, D:2 * D], ACT.Copy,
                                         scale=dinv[:, j:j + 1]).then_inc(s_scaled, 1)
                    if not last:
                        if j == 0:
                            odd_h(n + 1, 7)
                        elif j <= PAIRS:
                            x_high(n + 1, j - 1)

            over_graphs(act, graph)

        @block.gpsimd
        def _(pool):
            nc.gpsimd.memset(ident[:], 0.0).then_inc(ident_zero, 1)
            nc.gpsimd.memset(ident16[:], 0.0).then_inc(ident_zero, 1)
            nc.gpsimd.memset(half[:], -0.5).then_inc(half_set, 1)
            pool.wait_ge(ident_zero, 2)
            for m in (ident, ident16):
                nc.gpsimd.affine_select(out=m[:], in_=m[:], compare_op=ALU.not_equal, fill=1.0, base=0,
                                        pattern=[[-1, P]], channel_multiplier=1).then_inc(ident_set, 1)
            pool.wait_ge(half_set, 1)

            def output_power(n, group, size):
                lo = group % (K // size) * size if size < K else 0
                pool.wait_ge(veps2_set, n + 1 + (group if size < K else 0))
                nc.gpsimd.tensor_tensor(rstd2[:, lo:lo + size], veps2[:, lo:lo + size], half[:, 0:size],
                                        ALU.pow).then_inc(rstd2_set, 1)

            def graph(n, first, last):
                for j in range(K):
                    pool.wait_ge(u_hi, n * K + j + 1)
                    nc.gpsimd.tensor_tensor(mid[:, j, D:2 * D], whole[:, j % 2, :], mid[:, j, 0:D].bitcast(F32),
                                            ALU.subtract).then_inc(u_lo, 1)
                if not first:
                    output_power(n - 1, 0, K)
                for step in range(K + Q_LAG + 1):
                    j = step - Q_LAG - 1
                    if 0 <= j:
                        pool.wait_ge(q_copied, n * K + j + 1)
                        if j >= 2:
                            pool.wait_ge(q_whole, n * K + j - 1)
                        elif not first:
                            pool.wait_ge(s_set, n * K)
                        nc.gpsimd.tensor_tensor(add_lo[:, j % 2, :], scaled_lo[:, j % 2, :], bw_row[:],
                                                ALU.add).then_inc(q_beta, 1)
                    if 3 <= step <= K + 1 and step % 2:
                        i = (step - 3) // 2
                        pool.wait_ge(veps_set, n * PAIRS + i + 1)
                        nc.gpsimd.tensor_tensor(rstd[:, 2 * i:2 * i + 2], veps[:, 2 * i:2 * i + 2], half[:, 0:2],
                                                ALU.pow).then_inc(rstd_set, 1)
                    if 0 <= j:
                        pool.wait_ge(q_hi, n * K + j + 1)
                        nc.gpsimd.tensor_tensor(feat[:, j, D:2 * D], whole[:, j % 2, :],
                                                feat[:, j, 0:D].bitcast(F32), ALU.subtract).then_inc(q_lo, 1)
                for j in range(K):
                    pool.wait_ge(p_hi, n * K + j + 1)
                    nc.gpsimd.tensor_tensor(mid[:, j, D:2 * D], whole[:, j % 2, :], mid[:, j, 0:D].bitcast(F32),
                                            ALU.subtract).then_inc(p_lo, 1)
                pool.wait_ge(resid_set, 2 * (n + 1))
                for j in range(K):
                    pool.wait_ge(s_scaled, n * K + j + 1)
                    if j < 2:
                        pool.wait_ge(q_whole, n * K + K)
                    else:
                        pool.wait_ge(s_set, n * K + j - 1)
                    nc.gpsimd.tensor_tensor(add_lo[:, j % 2, :], scaled_lo[:, j % 2, :], resid[:, j, :],
                                            ALU.add).then_inc(s_resid, 1)
                    if last and j % 2 and j > 1:
                        output_power(n, j // 2 - 1, 2)
                if last:
                    output_power(n, PAIRS - 1, 2)

            over_graphs(pool, graph)

        @block.vector
        def _(dve):
            def set_h16(n, k):
                dve.wait_ge(adj_in[k % SLOTS], 16 * (2 * n + k // SLOTS + 1))
                nc.vector.tensor_scalar(H16[:, k, :], adj_sb[:, k % SLOTS, :], 0.0, None,
                                        ALU.not_equal).then_inc(h16_set, 1)

            def even_h(n, k):
                dve.wait_ge(h16_set, n * K + k + 1)
                nc.vector.tensor_copy(H[:, k, :], H16[:, k, :]).then_inc(h_even, 1)

            def x_low(n, i):
                dve.wait_ge(x_hi, n * PAIRS + i + 1)
                nc.vector.tensor_tensor(feat[:, 2 * i:2 * i + 2, D:2 * D], x_sb[:, 2 * i:2 * i + 2, :],
                                        feat[:, 2 * i:2 * i + 2, 0:D].bitcast(F32), ALU.subtract).then_inc(x_lo, 1)

            for k in range(SLOTS):
                set_h16(0, k)
                if k % 2 == 0:
                    even_h(0, k)
            for i in range(PAIRS):
                x_low(0, i)
            for k in range(SLOTS, K):
                set_h16(0, k)
                if k % 2 == 0:
                    even_h(0, k)
            dve.wait_ge(weights_in, 96)
            for b in range(HB):
                nc.vector.tensor_copy(beta_cols[:, b, :], bcol[:, b:b + 1].to_broadcast([P, P])).then_inc(beta_set, 1)
            dve.wait_ge(w_hi, 1)
            nc.vector.tensor_tensor(w1p[:, 1], w1_raw, w1p[:, 0].bitcast(F32), ALU.subtract).then_inc(w_lo, 1)

            def output_stats(n, j):
                dve.wait_ge(s_set, n * K + j + 1)
                nc.vector.bn_stats(stats2[:, j, :], ssum[:, j, :]).then_inc(bn2_set, 1)

            def output_aggregate(j):
                nc.vector.bn_aggr(mv2[:, j, :], stats2[:, j, :]).then_inc(mv2_set, 1)

            def output_epsilon(n, lo, size):
                dve.wait_ge(mv2_set, n * K + lo + size)
                nc.vector.tensor_scalar(veps2[:, lo:lo + size], mv2[:, lo:lo + size, 1], EPS, None,
                                        ALU.add).then_inc(veps2_set, 1)

            def output_pair(n, i, powers):
                dve.wait_ge(rstd2_set, powers)
                for j in (2 * i, 2 * i + 1):
                    nc.vector.tensor_scalar(ssum[:, j, :], ssum[:, j, :], mv2[:, j, 0:1], rstd2[:, j:j + 1],
                                            ALU.subtract, ALU.mult).then_inc(y_set, 1)

            def graph(n, first, last):
                def combine(j, scaled, done, bank):
                    dve.wait_ge(scaled, n * K + j + 1)
                    nc.vector.scalar_tensor_tensor(whole[:, j % 2, :], bank[:, 0:D], binv[:, j:j + 1],
                                                   scaled_lo[:, j % 2, :], ALU.mult, ALU.add).then_inc(done, 1)

                def row_sum(k):
                    if k > 0:
                        dve.wait_ge(dsum_set, n * K + k)
                    (dve.wait_ge(h_odd, n * PAIRS + k // 2 + 1) if k % 2
                     else dve.wait_ge(h_even, n * PAIRS + k // 2 + 1))
                    nc.vector.tensor_tensor_reduce(out=prod_junk, in0=H[:, k, :].bitcast(F32), in1=w_row[:],
                                                   scale=1.0, scalar=0.0, op0=ALU.mult, op1=ALU.add,
                                                   accum_out=dsum[:, k:k + 1]).then_inc(dsum_set, 1)

                if not first:
                    dve.wait_ge(tT_done, n * K)
                    dve.wait_ge(p_lo, n * K)
                dve.wait_ge(w_in, 16 * (n + 1))
                for j in range(K):
                    dve.wait_ge(ht_set, n * K + j + 1)
                    nc.vector.tensor_scalar(count1[:, j:j + 1], count[:, j:j + 1], 1.0, None,
                                            ALU.max).then_inc(count_set, 1)
                    dve.wait_ge(count_set, n * K + j + 1)
                    nc.vector.reciprocal(binv[:, j:j + 1], count1[:, j:j + 1]).then_inc(binv_set, 1)
                    if j < K - 2:
                        row_sum(j)
                    if j >= 2:
                        dve.wait_ge(u_lo, n * K + j - 1)
                    combine(j, u_scaled, u_whole, banks[6 + j % 2])

                def v_low(g):
                    h, b = g // DB, g % DB
                    dve.wait_ge(v_hi, n * DB * CH + g + 1)
                    nc.vector.tensor_tensor(vT[:, 1, b, h * BANK:(h + 1) * BANK], banks[g][:, :],
                                            vT[:, 0, b, h * BANK:(h + 1) * BANK].bitcast(F32),
                                            ALU.subtract).then_inc(v_lo, 1)

                if first:
                    dve.wait_ge(bw_done, 1)
                    nc.vector.tensor_copy(bw_row[:], banks[0][:, 0:D]).then_inc(bw_set, 1)
                    for b in range(HB):
                        nc.vector.tensor_scalar(w2_raw[:, b, :], w2_raw[:, b, :], gcol[:, b:b + 1], None,
                                                ALU.mult).then_inc(w2_scaled, 1)
                    dve.wait_ge(w2_scaled, HB)
                    dve.wait_ge(w_hi, 2)
                    nc.vector.tensor_tensor(w2p[:, :, D:2 * D], w2_raw, w2p[:, :, 0:D].bitcast(F32),
                                            ALU.subtract).then_inc(w_lo, 1)
                if not first:
                    for j in range(K):
                        if j > 0:
                            dve.wait_ge(bn2_set, (n - 1) * K + j)
                        output_stats(n - 1, j)
                        if j > 0:
                            output_aggregate(j - 1)
                    dve.wait_ge(bn2_set, n * K)
                row_sum(K - 2)
                if not first:
                    output_aggregate(K - 1)
                    output_epsilon(n - 1, 0, K)
                v_low(0)
                row_sum(K - 1)
                dve.wait_ge(dsum_set, (n + 1) * K)
                nc.vector.scalar_tensor_tensor(dsafe[:], dsum[:], 0.0, dsum[:], ALU.is_le,
                                               ALU.max).then_inc(dsafe_set, 1)
                dve.wait_ge(dsafe_set, n + 1)
                nc.vector.reciprocal(drec[:], dsafe[:]).then_inc(drec_set, 1)
                dve.wait_ge(drec_set, n + 1)
                nc.vector.scalar_tensor_tensor(dinv[:], dsum[:], 0.0, drec[:], ALU.is_gt,
                                               ALU.mult).then_inc(dinv_set, 1)
                if not first:
                    output_pair(n - 1, 0, n)
                v_low(1)
                if not first:
                    output_pair(n - 1, 1, n)
                    output_pair(n - 1, 2, n)
                v_low(2)
                if not first:
                    output_pair(n - 1, 3, n)
                v_low(3)

                dve.wait_ge(dinv_set, n + 1)
                def t_low(j):
                    dve.wait_ge(tT_hi, n * K + j + 1)
                    nc.vector.tensor_tensor(hidT[:, j % 2, 1].rearrange("p b m -> p (b m)"), banks[j % 2][:, :],
                                            hidT[:, j % 2, 0].rearrange("p b m -> p (b m)").bitcast(F32),
                                            ALU.subtract).then_inc(tT_lo, 1)

                for step in range(K + Q_LAG + 1):
                    j = step - T_LAG + 1
                    if 0 <= j < K:
                        dve.wait_ge(rstd_set, n * PAIRS + j // 2 + 1)
                        nc.vector.tensor_scalar(hid[:, j, :], hid[:, j, :], mv[:, j, 0:1], rstd[:, j:j + 1],
                                                ALU.subtract, ALU.mult).then_inc(t_set, 1)
                    if 1 < step <= K + 1:
                        dve.wait_ge(bn_set, n * K + step - 1)
                    if step < K:
                        if step < PAIRS and not first:
                            dve.wait_ge(y_out[step], 16 * n)
                        dve.wait_ge(z_done, n * K + step + 1)
                        nc.vector.scalar_tensor_tensor(hid[:, step, :], banks[4 + step % 4][:, :],
                                                       dinv[:, step:step + 1], b1_row[:],
                                                       ALU.mult, ALU.add).then_inc(z_set, 1)
                    elif step < K + T_LAG:
                        t_low(step - T_LAG)
                    if 1 < step <= K + 1:
                        j = step - 2
                        nc.vector.bn_aggr(mv[:, j, :], stats[:, j, :]).then_inc(mv_set, 1)
                        if j % 2:
                            dve.wait_ge(mv_set, n * K + j + 1)
                            nc.vector.tensor_scalar(veps[:, j - 1:j + 1], mv[:, j - 1:j + 1, 1], EPS, None,
                                                    ALU.add).then_inc(veps_set, 1)
                    if 0 < step <= K:
                        dve.wait_ge(relu_set, n * K + step)
                        nc.vector.bn_stats(stats[:, step - 1, :], hid[:, step - 1, :]).then_inc(bn_set, 1)
                    j = step - Q_LAG - 1
                    if 0 <= j:
                        dve.wait_ge(q_beta, n * K + j + 1)
                        if j < 2:
                            dve.wait_ge(u_lo, n * K + K)
                        else:
                            dve.wait_ge(q_lo, n * K + j - 1)
                        nc.vector.tensor_tensor(whole[:, j % 2, :], banks[2 + j % 2][:, 0:D], add_lo[:, j % 2, :],
                                                ALU.add).then_inc(q_whole, 1)
                    if T_LAG <= step < K:
                        t_low(step - T_LAG)

                def residual(i):
                    b = slice(i * K // 2, (i + 1) * K // 2)
                    nc.vector.scalar_tensor_tensor(resid[:, b, :], x_sb[:, b, :], 2.0,
                                                   b2_row[:].unsqueeze(1).to_broadcast([P, K // 2, D]),
                                                   ALU.mult, ALU.add).then_inc(resid_set, 1)

                if not first:
                    dve.wait_ge(s_resid, n * K)
                residual(0)
                if not last:
                    dve.wait_ge(z_done, n * K + K)
                    set_h16(n + 1, 0)
                dve.wait_ge(q_lo, n * K + K)
                for j in range(K):
                    if j >= 2:
                        dve.wait_ge(p_lo, n * K + j - 1)
                    combine(j, p_scaled, p_whole, banks[(4 + j) % 8])
                    if j == 0:
                        residual(1)
                    if not last and j + 1 < K:
                        set_h16(n + 1, j + 1)

                if not last:
                    dve.wait_ge(p_done, n * K + K)
                    even_h(n + 1, 0)
                    even_h(n + 1, 2)
                    even_h(n + 1, 4)
                for j in range(K):
                    if last and j > 0:
                        dve.wait_ge(bn2_set, n * K + j)
                    dve.wait_ge(s_resid, n * K + j + 1)
                    nc.vector.scalar_tensor_tensor(ssum[:, j, :], banks[j][:, 0:D], dinv[:, j:j + 1],
                                                   add_lo[:, j % 2, :], ALU.mult, ALU.add).then_inc(s_set, 1)
                    if not last:
                        if j == 0:
                            even_h(n + 1, 6)
                        elif 2 <= j < 2 + PAIRS:
                            x_low(n + 1, j - 2)
                    else:
                        if j > 0:
                            output_aggregate(j - 1)
                        if j > 0 and j % 2 == 0:
                            output_epsilon(n, j - 2, 2)
                        output_stats(n, j)
                        if j >= 4 and j % 2 == 0:
                            output_pair(n, j // 2 - 2, N - 1 + j // 2 - 1)
                if last:
                    output_pair(n, PAIRS - 2, N - 1 + PAIRS - 1)
                    dve.wait_ge(bn2_set, n * K + K)
                    output_aggregate(K - 1)
                    output_epsilon(n, K - 2, 2)
                    output_pair(n, PAIRS - 1, N - 1 + PAIRS)

            over_graphs(dve, graph)

        @block.tensor
        def _(pe):
            pe.wait_ge(ident_set, 2)

            def graph(n, first, last):
                def transpose_h(j):
                    if j >= 2:
                        pe.wait_ge(ht_set, n * K + j - 1)
                    elif not first:
                        pe.wait_ge(s_set, (n - 1) * K + 5 + j)
                    for k in range(K):
                        if j == 0:
                            pe.wait_ge(h16_set, n * K + k + 1)
                        mm = nc.tensor.transpose(banks[4 + j % 2][:, :].bitcast(BF16)[:, k * P:(k + 1) * P],
                                                 H16[:, k, j * P:(j + 1) * P], ident16[:])
                    mm.then_inc(ht_done, 1)

                transpose_h(0)
                transpose_h(1)
                pe.wait_ge(x_lo, PAIRS * (n + 1))
                pe.wait_ge(h_even, PAIRS * (n + 1))
                pe.wait_ge(h_odd, PAIRS * (n + 1))
                for j in range(K):
                    if j >= 2:
                        pe.wait_ge(u_whole, n * K + j - 1)
                    elif not first:
                        pe.wait_ge(s_set, (n - 1) * K + 7 + j)
                    for k in range(K):
                        mm = nc.tensor.matmul(banks[6 + j % 2][:, :], H[:, k, j * P:(j + 1) * P], feat[:, k, :],
                                              start=(k == 0), stop=(k == K - 1))
                    mm.then_inc(u_done, 1)
                    if j + 2 < K:
                        transpose_h(j + 2)
                if first:
                    pe.wait_ge(beta_set, HB)
                    pe.wait_ge(weights_in, 96)
                    for b in range(HB):
                        mm = nc.tensor.matmul(banks[0][:, 0:D], beta_cols[:, b, :], w2_raw[:, b, :],
                                              start=(b == 0), stop=(b == HB - 1))
                    mm.then_inc(bw_done, 1)
                if first:
                    pe.wait_ge(bw_set, 1)
                for g in range(DB * CH):
                    h, b = g // DB, g % DB
                    for k in range(K):
                        for part in range(2):
                            if g == 0:
                                pe.wait_ge((u_hi, u_lo)[part], n * K + k + 1)
                                pe.wait_ge(ht_set, n * K + k + 1)
                            mm = nc.tensor.matmul(banks[g][:, :], mid[:, k, part * D + b * P:part * D + (b + 1) * P],
                                                  HT[:, k, h * BANK:(h + 1) * BANK],
                                                  start=(k == 0 and part == 0), stop=(k == K - 1 and part == 1))
                    mm.then_inc(v_done, 1)
                if first:
                    pe.wait_ge(w_lo, 2)
                for step in range(K + Q_LAG):
                    j = step
                    if j < K:
                        if j % 4 == 0:
                            pe.wait_ge(v_lo, n * DB * CH + (j // 4 + 1) * DB)
                        if j >= 4:
                            pe.wait_ge(z_set, n * K + j - 3)
                        for b in range(DB):
                            for part in range(2):
                                for wpart in range(2):
                                    mm = nc.tensor.matmul(banks[4 + j % 4][:, :], vT[:, part, b, j * P:(j + 1) * P],
                                                          w1p[:, wpart, b, :], start=(b + part + wpart == 0),
                                                          stop=(b + part + wpart == DB + 1))
                        mm.then_inc(z_done, 1)
                    j = step - T_LAG
                    if 0 <= j < K:
                        pe.wait_ge(t_set, n * K + j + 1)
                        if j >= 2:
                            pe.wait_ge(tT_lo, n * K + j - 1)
                        for b in range(HB):
                            mm = nc.tensor.transpose(banks[j % 2][:, b * P:(b + 1) * P],
                                                     hid[:, j, b * P:(b + 1) * P], ident[:])
                        mm.then_inc(tT_done, 1)
                    j = step - Q_LAG
                    if 0 <= j:
                        pe.wait_ge(tT_lo, n * K + j + 1)
                        if j >= 2:
                            pe.wait_ge(q_whole, n * K + j - 1)
                        for b in range(HB):
                            for part in range(2):
                                mm = nc.tensor.matmul(banks[2 + j % 2][:, :], hidT[:, j % 2, part, b, :],
                                                      w2p[:, b, :], start=(b + part == 0), stop=(b + part == HB))
                        mm.then_inc(q_done, 1)
                for j, blocks in P_ORDER:
                    for k in blocks:
                        if j < 2:
                            pe.wait_ge(q_lo, n * K + k + 1)
                        mm = nc.tensor.matmul(banks[(4 + j) % 8][:, :], H[:, k, j * P:(j + 1) * P],
                                              feat[:, k, :], start=(k == 0), stop=(k == K - 1))
                        if k == K - 1:
                            mm.then_inc(p_done, 1)
                for j, blocks in P_ORDER:
                    for k in blocks:
                        if j < 2:
                            pe.wait_ge(p_lo, n * K + k + 1)
                        if k == 0 and j < 4:
                            pe.wait_ge(p_whole, n * K + 5 + j)
                        mm = nc.tensor.matmul(banks[j][:, :], HT[:, k, j * P:(j + 1) * P],
                                              mid[:, k, :], start=(k == 0), stop=(k == K - 1))
                        if k == K - 1:
                            mm.then_inc(s_done, 1)

            over_graphs(pe, graph)


def kernel(**inputs):
    import numpy as np
    import concourse.bacc as bacc
    from concourse.bass_utils import run_bass_kernel_spmd

    laid_out = {
        "x": inputs["x"], "adj": inputs["adj"],
        "w1t": np.asarray(inputs["L0_gnn_W1"]).T, "b1": inputs["L0_gnn_b1"],
        "gamma": np.asarray(inputs["L0_gnn_gamma"]).reshape(-1, P).T,
        "beta": np.asarray(inputs["L0_gnn_beta"]).reshape(-1, P).T,
        "w2t": np.asarray(inputs["L0_gnn_W2"]).T, "b2": inputs["L0_gnn_b2"],
    }
    nc = bacc.Bacc("TRN2", target_bir_lowering=False, num_devices=1)
    arrays, args = {}, []
    for name, value in laid_out.items():
        a = np.ascontiguousarray(value)
        arrays[f"in_{name}"] = a
        args.append(nc.dram_tensor(f"in_{name}", a.shape, mybir.dt.from_np(a.dtype), kind="ExternalInput").ap())
    shape = arrays["in_x"].shape
    args.append(nc.dram_tensor("out_0", shape, F32, kind="ExternalOutput").ap())
    graph_kernel(nc, *args)
    result = run_bass_kernel_spmd(nc, [arrays], core_ids=[0])
    return result.results[0]["out_0"]
```

```python
from contextlib import ExitStack

import concourse.bass as bass
from concourse import mybir

P = 128
F32 = mybir.dt.float32
F32R = mybir.dt.float32r
BF16 = mybir.dt.bfloat16
ALU = mybir.AluOpType
ACT = mybir.ActivationFunctionType
EPS = 1e-5
SLOTS = 4
BANK = 512
HT_SCALAR = (0, 1, 3, 5)
HT_VECTOR = (2, 4, 6, 7)
T_LAG = 5
Q_LAG = 6


def graph_kernel(nc: bass.Bass, x, adj, w1t, b1, gamma, beta, w2t, b2, out):
    N, C, D = x.shape
    DH = w1t.shape[1]
    K = C // P
    DB = D // P
    HB = DH // P
    CH = C // BANK
    PAIRS = K // 2
    EARLY_SUMS = K // 2
    assert C == K * P and D * 2 == BANK and DH == BANK and K == 8 and SLOTS * 2 == K and N >= 3

    adj_rows = adj.rearrange("n (p k) e -> n p k e", k=K)
    x_rows = x.rearrange("n (p k) d -> n p k d", k=K)
    out_rows = out.rearrange("n (p k) d -> n p k d", k=K)

    with ExitStack() as ctx:
        def sb(name, shape, dt=F32):
            return ctx.enter_context(nc.sbuf_tensor(name, shape, dt))

        def sem(name):
            return ctx.enter_context(nc.semaphore(name))

        adj_sb = sb("adj_sb", [P, SLOTS, C])
        H = sb("H", [P, K, C], F32R)
        HT = sb("HT", [P, K, C], F32R)
        x_sb = sb("x_sb", [P, K, D])
        resid = sb("resid", [P, K, D])
        feat = sb("feat", [P, K, 2 * D], F32R)
        mid = sb("mid", [P, K, 2 * D], F32R)
        H16 = sb("H16", [P, K, C], BF16)
        shared = nc.sbuf_base
        HT16 = sb("HT16", [P, K, C], BF16)
        vT = nc.alloc_sbuf_tensor_at("vT", [P, DB, C], F32, offset=shared)
        hid = sb("hid", [P, K, DH])
        hidT = sb("hidT", [P, 2, HB, P])
        w1 = sb("w1", [P, DB, DH])
        w2 = sb("w2", [P, HB, D])
        w_row = sb("w_row", [P, C])
        b1_row = sb("b1_row", [P, DH])
        b2_row = sb("b2_row", [P, D])
        bw_row = sb("bw_row", [P, D])
        ident = sb("ident", [P, P])
        scaled_lo = sb("scaled_lo", [P, 2, D])
        add_lo = sb("add_lo", [P, 2, D])
        whole = sb("whole", [P, 2, D])
        gcol = sb("gcol", [P, HB])
        bcol = sb("bcol", [P, HB])
        half = sb("half", [P, K])
        count = sb("count", [P, K])
        count1 = sb("count1", [P, K])
        binv = sb("binv", [P, K])
        dsum = sb("dsum", [P, K])
        dsafe = sb("dsafe", [P, K])
        drec = sb("drec", [P, K])
        dinv = sb("dinv", [P, K])
        stats = sb("stats", [P, K, 6])
        mv = sb("mv", [P, K, 2])
        veps = sb("veps", [P, K])
        rstd = sb("rstd", [P, K])
        stats2 = sb("stats2", [P, K, 6])
        mv2 = sb("mv2", [P, K, 2])
        veps2 = sb("veps2", [P, K])
        rstd2 = sb("rstd2", [P, K])
        banks = [ctx.enter_context(nc.psum_tensor(f"bank{i}", [P, BANK], F32)) for i in range(8)]

        beta_cols = hid[:, 0, :].rearrange("p (b m) -> p b m", b=HB)
        ssum = hid[:, 0:K // 2, :].rearrange("p a (b d) -> p (a b) d", d=D)
        prod_junk = hid[:, 6:8, :].rearrange("p a h -> p (a h)")

        adj_in = [sem(f"adj_in{i}") for i in range(SLOTS)]
        x_in = [sem(f"x_in{i}") for i in range(PAIRS)]
        w_in, weights_in = sem("w_in"), sem("weights_in")
        y_out = [sem(f"y_out{i}") for i in range(PAIRS)]
        ident_zero, ident_set, half_set = sem("ident_zero"), sem("ident_set"), sem("half_set")
        w2_scaled, beta_set = sem("w2_scaled"), sem("beta_set")
        bw_done, bw_set = sem("bw_done"), sem("bw_set")
        h16_set, h_even, h_odd = sem("h16_set"), sem("h_even"), sem("h_odd")
        ht16_in, ht_scalar, ht_vector = sem("ht16_in"), sem("ht_scalar"), sem("ht_vector")
        x_hi, x_lo, resid_set = sem("x_hi"), sem("x_lo"), sem("resid_set")
        count_set, binv_set = sem("count_set"), sem("binv_set")
        dsum_set, dsafe_set, drec_set, dinv_set = sem("dsum_set"), sem("dsafe_set"), sem("drec_set"), sem("dinv_set")
        u_done, v_done, z_done, tT_done = sem("u_done"), sem("v_done"), sem("z_done"), sem("tT_done")
        q_done, p_done, s_done = sem("q_done"), sem("p_done"), sem("s_done")
        u_scaled, u_whole, u_hi, u_lo = sem("u_scaled"), sem("u_whole"), sem("u_hi"), sem("u_lo")
        p_scaled, p_whole, p_hi, p_lo = sem("p_scaled"), sem("p_whole"), sem("p_hi"), sem("p_lo")
        v_set = sem("v_set")
        z_set, relu_set, bn_set, mv_set = sem("z_set"), sem("relu_set"), sem("bn_set"), sem("mv_set")
        veps_set, rstd_set, t_set = sem("veps_set"), sem("rstd_set"), sem("t_set")
        tT_set = sem("tT_set")
        q_whole, q_hi, q_lo = sem("q_whole"), sem("q_hi"), sem("q_lo")
        s_scaled, s_resid, s_set = sem("s_scaled"), sem("s_resid"), sem("s_set")
        bn2_set, mv2_set, veps2_set, rstd2_set, y_set = (sem("bn2_set"), sem("mv2_set"),
                                                         sem("veps2_set"), sem("rstd2_set"), sem("y_set"))

        Q_BANK = [2, 3, 4, 5, 6, 7, 2, 3]
        EARLY = K - 2
        P_ORDER = ([(j, range(EARLY)) for j in range(4)] + [(j, range(EARLY, K)) for j in range(4)]
                   + [(j, range(K)) for j in range(4, K)])

        def u_bank(j, first):
            return j if first else 4 + j % 4

        def over_graphs(eng, body):
            body(0, True, False)
            with eng.Fori(0, N - 2) as m:
                body(m + 1, False, False)
            body(N - 1, False, True)

        block = ctx.enter_context(nc.Block())

        @block.sync
        def _(sp):
            def load_adj(n, k):
                sp.dma_start(adj_sb[:, k % SLOTS, :], adj_rows[n, :, k, :]).then_inc(adj_in[k % SLOTS], 16)

            def store_result(n):
                for i in range(PAIRS):
                    sp.wait_ge(y_set, n * K + 2 * i + 2)
                    sp.dma_start(out_rows[n, :, 2 * i:2 * i + 2, :],
                                 ssum[:, 2 * i:2 * i + 2, :]).then_inc(y_out[i], 16)

            def load_x(n, i):
                sp.dma_start(x_sb[:, 2 * i:2 * i + 2, :], x_rows[n, :, 2 * i:2 * i + 2, :]).then_inc(x_in[i], 16)

            def transpose_h(k):
                sp.dma_start(HT16[:, :, k * P:(k + 1) * P], H16[:, k, :], transpose=True).then_inc(ht16_in, 16)

            for k in range(K):
                if k >= SLOTS:
                    sp.wait_ge(h16_set, k - SLOTS + 1)
                load_adj(0, k)
                if k % 2 == 0:
                    load_x(0, k // 2)
            for k in range(K):
                if k >= K - SLOTS:
                    sp.wait_ge(h16_set, k + 1)
                transpose_h(k)
            sp.dma_start(w_row[:], adj[0, 0, :].partition_broadcast(P)).then_inc(w_in, 16)
            sp.dma_start(bcol[:], beta).then_inc(weights_in, 16)
            sp.dma_start(gcol[:], gamma).then_inc(weights_in, 16)
            sp.dma_start(w2[:], w2t.rearrange("(b p) d -> p b d", p=P)).then_inc(weights_in, 16)
            sp.dma_start(w1[:], w1t.rearrange("(b p) h -> p b h", p=P)).then_inc(weights_in, 16)
            sp.dma_start(b1_row[:], b1.partition_broadcast(P)).then_inc(weights_in, 16)
            sp.dma_start(b2_row[:], b2.partition_broadcast(P)).then_inc(weights_in, 16)

            def graph(n, first, last):
                if not last:
                    for k in range(SLOTS):
                        load_adj(n + 1, k)
                    sp.wait_ge(dsum_set, (n + 1) * K)
                    sp.dma_start(w_row[:], adj[n + 1, 0, :].partition_broadcast(P)).then_inc(w_in, 16)
                if not first:
                    store_result(n - 1)
                if not last:
                    for k in range(SLOTS, K):
                        sp.wait_ge(h16_set, (n + 1) * K + k - SLOTS + 1)
                        load_adj(n + 1, k)
                        transpose_h(k - SLOTS)
                    for i in range(PAIRS):
                        sp.wait_ge(h16_set, (n + 1) * K + K - SLOTS + i + 1)
                        load_x(n + 1, i)
                        transpose_h(K - SLOTS + i)
                else:
                    store_result(n)

            over_graphs(sp, graph)
            for i in range(PAIRS):
                sp.wait_ge(y_out[i], 16 * N)

        @block.scalar
        def _(act):
            def odd_h(n, k):
                act.wait_ge(h16_set, n * K + k + 1)
                nc.scalar.activation(H[:, k, :], H16[:, k, :], ACT.Copy).then_inc(h_odd, 1)

            def x_high(n, i):
                act.wait_ge(x_in[i], 16 * (n + 1))
                nc.scalar.activation(feat[:, 2 * i:2 * i + 2, 0:D], x_sb[:, 2 * i:2 * i + 2, :],
                                     ACT.Copy).then_inc(x_hi, 1)

            for i in range(PAIRS):
                x_high(0, i)
                odd_h(0, 2 * i + 1)

            def graph(n, first, last):
                def store_ht(j):
                    nc.scalar.activation(HT[:, j, :], HT16[:, j, :], ACT.Copy,
                                         accum_out=count[:, j:j + 1]).then_inc(ht_scalar, 1)

                if not first:
                    act.wait_ge(s_done, n * K)
                    act.wait_ge(binv_set, n * K)
                act.wait_ge(ht16_in, 16 * K * (n + 1))
                for j in HT_SCALAR[:3]:
                    store_ht(j)
                def scale_u_lo(j):
                    act.wait_ge(u_done, n * K + j + 1)
                    act.wait_ge(binv_set, n * K + j + 1)
                    if j >= 2:
                        act.wait_ge(u_whole, n * K + j - 1)
                    elif not first:
                        act.wait_ge(s_resid, n * K)
                    nc.scalar.activation(scaled_lo[:, j % 2, :], banks[u_bank(j, first)][:, D:2 * D], ACT.Copy,
                                         scale=binv[:, j:j + 1]).then_inc(u_scaled, 1)

                scale_u_lo(0)
                store_ht(HT_SCALAR[3])
                for j in range(K):
                    if j + 1 < K:
                        scale_u_lo(j + 1)
                    act.wait_ge(u_whole, n * K + j + 1)
                    nc.scalar.activation(mid[:, j, 0:D], whole[:, j % 2, :], ACT.Copy).then_inc(u_hi, 1)
                for g in range(DB * CH):
                    h, b = g // DB, g % DB
                    act.wait_ge(v_done, n * DB * CH + g + 1)
                    nc.scalar.activation(vT[:, b, h * BANK:(h + 1) * BANK], banks[g][:, :],
                                         ACT.Copy).then_inc(v_set, 1)
                for step in range(K + Q_LAG + 1):
                    j = step - Q_LAG - 1
                    i = step - T_LAG
                    if 0 <= i < K:
                        act.wait_ge(tT_done, n * K + i + 1)
                        if i >= 2:
                            act.wait_ge(q_done, n * K + i - 1)
                        nc.scalar.activation(hidT[:, i % 2].rearrange("p b m -> p (b m)"), banks[i % 2][:, :],
                                             ACT.Copy).then_inc(tT_set, 1)
                    if step < K:
                        act.wait_ge(z_set, n * K + step + 1)
                        nc.scalar.activation(hid[:, step, :], hid[:, step, :], ACT.Relu).then_inc(relu_set, 1)
                    if 0 <= j:
                        act.wait_ge(q_whole, n * K + j + 1)
                        nc.scalar.activation(feat[:, j, 0:D], whole[:, j % 2, :], ACT.Copy).then_inc(q_hi, 1)
                def scale_p_lo(j):
                    act.wait_ge(p_done, n * K + j + 1)
                    if j < 2:
                        act.wait_ge(u_whole, n * K + K)
                    else:
                        act.wait_ge(p_whole, n * K + j - 1)
                    nc.scalar.activation(scaled_lo[:, j % 2, :], banks[(4 + j) % 8][:, D:2 * D], ACT.Copy,
                                         scale=binv[:, j:j + 1]).then_inc(p_scaled, 1)

                scale_p_lo(0)
                for j in range(K):
                    if j + 1 < K:
                        scale_p_lo(j + 1)
                    act.wait_ge(p_whole, n * K + j + 1)
                    nc.scalar.activation(mid[:, j, 0:D], whole[:, j % 2, :], ACT.Copy).then_inc(p_hi, 1)
                if not last:
                    odd_h(n + 1, 1)
                    odd_h(n + 1, 3)
                    odd_h(n + 1, 5)
                for j in range(K):
                    act.wait_ge(s_done, n * K + j + 1)
                    if j < 2:
                        act.wait_ge(p_whole, n * K + K)
                    else:
                        act.wait_ge(s_resid, n * K + j - 1)
                    nc.scalar.activation(scaled_lo[:, j % 2, :], banks[j][:, D:2 * D], ACT.Copy,
                                         scale=dinv[:, j:j + 1]).then_inc(s_scaled, 1)
                    if not last:
                        if j == 0:
                            odd_h(n + 1, 7)
                        elif j <= PAIRS:
                            x_high(n + 1, j - 1)

            over_graphs(act, graph)

        @block.gpsimd
        def _(pool):
            nc.gpsimd.memset(ident[:], 0.0).then_inc(ident_zero, 1)
            nc.gpsimd.memset(half[:], -0.5).then_inc(half_set, 1)
            pool.wait_ge(ident_zero, 1)
            nc.gpsimd.affine_select(out=ident[:], in_=ident[:], compare_op=ALU.not_equal, fill=1.0, base=0,
                                    pattern=[[-1, P]], channel_multiplier=1).then_inc(ident_set, 1)
            pool.wait_ge(half_set, 1)

            def output_power(n, group, size):
                lo = group % (K // size) * size if size < K else 0
                pool.wait_ge(veps2_set, n + 1 + (group if size < K else 0))
                nc.gpsimd.tensor_tensor(rstd2[:, lo:lo + size], veps2[:, lo:lo + size], half[:, 0:size],
                                        ALU.pow).then_inc(rstd2_set, 1)

            def graph(n, first, last):
                for j in range(K):
                    pool.wait_ge(u_hi, n * K + j + 1)
                    nc.gpsimd.tensor_tensor(mid[:, j, D:2 * D], whole[:, j % 2, :], mid[:, j, 0:D].bitcast(F32),
                                            ALU.subtract).then_inc(u_lo, 1)
                if not first:
                    output_power(n - 1, 0, K)
                for step in range(K + Q_LAG + 1):
                    j = step - Q_LAG - 1
                    if 3 <= step <= K + 1 and step % 2:
                        i = (step - 3) // 2
                        pool.wait_ge(veps_set, n * PAIRS + i + 1)
                        nc.gpsimd.tensor_tensor(rstd[:, 2 * i:2 * i + 2], veps[:, 2 * i:2 * i + 2], half[:, 0:2],
                                                ALU.pow).then_inc(rstd_set, 1)
                    if 0 <= j:
                        pool.wait_ge(q_hi, n * K + j + 1)
                        nc.gpsimd.tensor_tensor(feat[:, j, D:2 * D], whole[:, j % 2, :],
                                                feat[:, j, 0:D].bitcast(F32), ALU.subtract).then_inc(q_lo, 1)
                for j in range(K):
                    pool.wait_ge(p_hi, n * K + j + 1)
                    nc.gpsimd.tensor_tensor(mid[:, j, D:2 * D], whole[:, j % 2, :], mid[:, j, 0:D].bitcast(F32),
                                            ALU.subtract).then_inc(p_lo, 1)
                pool.wait_ge(resid_set, (n + 1) * K)
                for j in range(K):
                    pool.wait_ge(s_scaled, n * K + j + 1)
                    if j >= 2:
                        pool.wait_ge(s_set, n * K + j - 1)
                    elif not first:
                        pool.wait_ge(s_set, n * K)
                    nc.gpsimd.tensor_tensor(add_lo[:, j % 2, :], scaled_lo[:, j % 2, :], resid[:, j, :],
                                            ALU.add).then_inc(s_resid, 1)
                    if last and j % 2 and j > 1:
                        output_power(n, j // 2 - 1, 2)
                if last:
                    output_power(n, PAIRS - 1, 2)

            over_graphs(pool, graph)

        @block.vector
        def _(dve):
            def set_h16(n, k):
                dve.wait_ge(adj_in[k % SLOTS], 16 * (2 * n + k // SLOTS + 1))
                nc.vector.tensor_scalar(H16[:, k, :], adj_sb[:, k % SLOTS, :], 0.0, None,
                                        ALU.not_equal).then_inc(h16_set, 1)

            def even_h(n, k):
                dve.wait_ge(h16_set, n * K + k + 1)
                nc.vector.tensor_copy(H[:, k, :], H16[:, k, :]).then_inc(h_even, 1)

            def x_low(n, i):
                dve.wait_ge(x_hi, n * PAIRS + i + 1)
                nc.vector.tensor_tensor(feat[:, 2 * i:2 * i + 2, D:2 * D], x_sb[:, 2 * i:2 * i + 2, :],
                                        feat[:, 2 * i:2 * i + 2, 0:D].bitcast(F32), ALU.subtract).then_inc(x_lo, 1)

            for k in range(K):
                set_h16(0, k)
                if k % 2 == 0:
                    even_h(0, k)
                    x_low(0, k // 2)

            def row_sum(n, k):
                if k > 0:
                    dve.wait_ge(dsum_set, n * K + k)
                dve.wait_ge(h16_set, n * K + k + 1)
                nc.vector.tensor_tensor_reduce(out=prod_junk, in0=H16[:, k, :], in1=w_row[:],
                                               scale=1.0, scalar=0.0, op0=ALU.mult, op1=ALU.add,
                                               accum_out=dsum[:, k:k + 1]).then_inc(dsum_set, 1)

            def output_stats(n, j):
                dve.wait_ge(s_set, n * K + j + 1)
                nc.vector.bn_stats(stats2[:, j, :], ssum[:, j, :]).then_inc(bn2_set, 1)

            def output_aggregate(j):
                nc.vector.bn_aggr(mv2[:, j, :], stats2[:, j, :]).then_inc(mv2_set, 1)

            def output_epsilon(n, lo, size):
                dve.wait_ge(mv2_set, n * K + lo + size)
                nc.vector.tensor_scalar(veps2[:, lo:lo + size], mv2[:, lo:lo + size, 1], EPS, None,
                                        ALU.add).then_inc(veps2_set, 1)

            def output_pair(i, powers):
                dve.wait_ge(rstd2_set, powers)
                for j in (2 * i, 2 * i + 1):
                    nc.vector.tensor_scalar(ssum[:, j, :], ssum[:, j, :], mv2[:, j, 0:1], rstd2[:, j:j + 1],
                                            ALU.subtract, ALU.mult).then_inc(y_set, 1)

            def graph(n, first, last):
                def combine(j, scaled, done, bank):
                    dve.wait_ge(scaled, n * K + j + 1)
                    nc.vector.scalar_tensor_tensor(whole[:, j % 2, :], bank[:, 0:D], binv[:, j:j + 1],
                                                   scaled_lo[:, j % 2, :], ALU.mult, ALU.add).then_inc(done, 1)

                def store_ht(j):
                    nc.vector.tensor_scalar(HT[:, j, :], HT16[:, j, :], 1.0, 0.0, ALU.mult, ALU.add,
                                            accum_out=count[:, j:j + 1]).then_inc(ht_vector, 1)

                def set_b(j):
                    if j in HT_SCALAR:
                        dve.wait_ge(ht_scalar, n * PAIRS + HT_SCALAR.index(j) + 1)
                    else:
                        dve.wait_ge(ht_vector, n * PAIRS + HT_VECTOR.index(j) + 1)
                    nc.vector.tensor_scalar(count1[:, j:j + 1], count[:, j:j + 1], 1.0, None,
                                            ALU.max).then_inc(count_set, 1)
                    dve.wait_ge(count_set, n * K + j + 1)
                    nc.vector.reciprocal(binv[:, j:j + 1], count1[:, j:j + 1]).then_inc(binv_set, 1)

                if not first:
                    dve.wait_ge(p_lo, n * K)
                    dve.wait_ge(s_done, n * K)
                dve.wait_ge(ht16_in, 16 * K * (n + 1))
                store_ht(HT_VECTOR[0])
                set_b(0)
                set_b(1)
                store_ht(HT_VECTOR[1])
                for j in range(K):
                    if j >= 2:
                        dve.wait_ge(u_lo, n * K + j - 1)
                    combine(j, u_scaled, u_whole, banks[u_bank(j, first)])
                    if j in (1, 3):
                        store_ht(HT_VECTOR[2 + j // 2])
                    if j + 2 < K:
                        set_b(j + 2)

                if first:
                    dve.wait_ge(weights_in, 96)
                    for b in range(HB):
                        nc.vector.tensor_copy(beta_cols[:, b, :],
                                              bcol[:, b:b + 1].to_broadcast([P, P])).then_inc(beta_set, 1)
                if not first:
                    for j in range(K):
                        if j > 0:
                            dve.wait_ge(bn2_set, (n - 1) * K + j)
                        output_stats(n - 1, j)
                        if j > 0:
                            output_aggregate(j - 1)
                    dve.wait_ge(bn2_set, n * K)
                if first:
                    dve.wait_ge(w_in, 16)
                for k in range(0 if first else EARLY_SUMS, K):
                    row_sum(n, k)
                    if k == K - 2 and not first:
                        output_aggregate(K - 1)
                        output_epsilon(n - 1, 0, K)
                dve.wait_ge(dsum_set, (n + 1) * K)
                nc.vector.scalar_tensor_tensor(dsafe[:], dsum[:], 0.0, dsum[:], ALU.is_le,
                                               ALU.max).then_inc(dsafe_set, 1)
                dve.wait_ge(dsafe_set, n + 1)
                nc.vector.reciprocal(drec[:], dsafe[:]).then_inc(drec_set, 1)
                dve.wait_ge(drec_set, n + 1)
                nc.vector.scalar_tensor_tensor(dinv[:], dsum[:], 0.0, drec[:], ALU.is_gt,
                                               ALU.mult).then_inc(dinv_set, 1)
                if first:
                    dve.wait_ge(bw_done, 1)
                    nc.vector.tensor_copy(bw_row[:], banks[6][:, 0:D]).then_inc(bw_set, 1)
                    for b in range(HB):
                        nc.vector.tensor_scalar(w2[:, b, :], w2[:, b, :], gcol[:, b:b + 1], None,
                                                ALU.mult).then_inc(w2_scaled, 1)
                else:
                    for i in range(PAIRS):
                        output_pair(i, n)

                dve.wait_ge(dinv_set, n + 1)
                for step in range(K + Q_LAG + 1):
                    if K <= step <= K + 1:
                        dve.wait_ge(bn_set, n * K + step - 1)
                    j = step - T_LAG + 1
                    if 0 <= j < K:
                        dve.wait_ge(rstd_set, n * PAIRS + j // 2 + 1)
                        nc.vector.tensor_scalar(hid[:, j, :], hid[:, j, :], mv[:, j, 0:1], rstd[:, j:j + 1],
                                                ALU.subtract, ALU.mult).then_inc(t_set, 1)
                    if 1 < step < K:
                        dve.wait_ge(bn_set, n * K + step - 1)
                    if step < K:
                        if step < PAIRS and not first:
                            dve.wait_ge(y_out[step], 16 * n)
                        dve.wait_ge(z_done, n * K + step + 1)
                        nc.vector.scalar_tensor_tensor(hid[:, step, :], banks[4 + step % 4][:, :],
                                                       dinv[:, step:step + 1], b1_row[:],
                                                       ALU.mult, ALU.add).then_inc(z_set, 1)
                    if 1 < step <= K + 1:
                        j = step - 2
                        nc.vector.bn_aggr(mv[:, j, :], stats[:, j, :]).then_inc(mv_set, 1)
                        if j % 2:
                            dve.wait_ge(mv_set, n * K + j + 1)
                            nc.vector.tensor_scalar(veps[:, j - 1:j + 1], mv[:, j - 1:j + 1, 1], EPS, None,
                                                    ALU.add).then_inc(veps_set, 1)
                    if 0 < step <= K:
                        dve.wait_ge(relu_set, n * K + step)
                        nc.vector.bn_stats(stats[:, step - 1, :], hid[:, step - 1, :]).then_inc(bn_set, 1)
                    j = step - Q_LAG - 1
                    if 0 <= j:
                        dve.wait_ge(q_done, n * K + j + 1)
                        if j < 2:
                            dve.wait_ge(u_lo, n * K + K)
                        else:
                            dve.wait_ge(q_lo, n * K + j - 1)
                        nc.vector.tensor_tensor(whole[:, j % 2, :], banks[Q_BANK[j]][:, 0:D], bw_row[:],
                                                ALU.add).then_inc(q_whole, 1)

                def residual(i):
                    b = slice(i * K // 2, (i + 1) * K // 2)
                    nc.vector.scalar_tensor_tensor(resid[:, b, :], x_sb[:, b, :], 2.0,
                                                   b2_row[:].unsqueeze(1).to_broadcast([P, K // 2, D]),
                                                   ALU.mult, ALU.add).then_inc(resid_set, K // 2)

                if not first:
                    dve.wait_ge(s_resid, n * K)
                if not last:
                    dve.wait_ge(ht16_in, 16 * K * (n + 1))
                    dve.wait_ge(z_done, n * K + K)
                    for k in range(SLOTS):
                        set_h16(n + 1, k)
                residual(0)
                residual(1)
                dve.wait_ge(q_lo, n * K + K)
                dve.wait_ge(resid_set, n * K + K)
                for j in range(K):
                    if j >= 2:
                        dve.wait_ge(p_lo, n * K + j - 1)
                    combine(j, p_scaled, p_whole, banks[(4 + j) % 8])
                    if not last and 2 <= j < 2 + K - SLOTS:
                        set_h16(n + 1, j + SLOTS - 2)

                if not last:
                    dve.wait_ge(p_done, n * K + K)
                    even_h(n + 1, 0)
                    even_h(n + 1, 2)
                    even_h(n + 1, 4)
                    dve.wait_ge(w_in, 16 * (n + 2))
                    row_sum(n + 1, 0)
                    row_sum(n + 1, 1)
                for j in range(K):
                    if last and j > 0:
                        dve.wait_ge(bn2_set, n * K + j)
                    dve.wait_ge(s_resid, n * K + j + 1)
                    nc.vector.scalar_tensor_tensor(ssum[:, j, :], banks[j][:, 0:D], dinv[:, j:j + 1],
                                                   add_lo[:, j % 2, :], ALU.mult, ALU.add).then_inc(s_set, 1)
                    if not last:
                        if j == 0:
                            even_h(n + 1, 6)
                        elif 2 <= j < 2 + PAIRS:
                            x_low(n + 1, j - 2)
                        if 5 <= j < 3 + EARLY_SUMS:
                            row_sum(n + 1, j - 3)
                    else:
                        if j > 0:
                            output_aggregate(j - 1)
                        if j > 0 and j % 2 == 0:
                            output_epsilon(n, j - 2, 2)
                        output_stats(n, j)
                        if j >= 4 and j % 2 == 0:
                            output_pair(j // 2 - 2, N - 1 + j // 2 - 1)
                if last:
                    output_pair(PAIRS - 2, N - 1 + PAIRS - 1)
                    dve.wait_ge(bn2_set, n * K + K)
                    output_aggregate(K - 1)
                    output_epsilon(n, K - 2, 2)
                    output_pair(PAIRS - 1, N - 1 + PAIRS)

            over_graphs(dve, graph)

        @block.tensor
        def _(pe):
            pe.wait_ge(ident_set, 1)

            def graph(n, first, last):
                if first:
                    for k in range(K):
                        pe.wait_ge(x_lo, k // 2 + 1)
                        pe.wait_ge((h_even, h_odd)[k % 2], k // 2 + 1)
                        for j in range(K):
                            mm = nc.tensor.matmul(banks[u_bank(j, first)][:, :], H[:, k, j * P:(j + 1) * P],
                                                  feat[:, k, :], start=(k == 0), stop=(k == K - 1))
                            if k == K - 1:
                                mm.then_inc(u_done, 1)
                else:
                    pe.wait_ge(x_lo, PAIRS * (n + 1))
                    pe.wait_ge(h_even, PAIRS * (n + 1))
                    pe.wait_ge(h_odd, PAIRS * (n + 1))
                    for j in range(K):
                        if j >= 4:
                            pe.wait_ge(u_whole, n * K + j - 3)
                        else:
                            pe.wait_ge(s_set, (n - 1) * K + 5 + j)
                        for k in range(K):
                            mm = nc.tensor.matmul(banks[u_bank(j, first)][:, :], H[:, k, j * P:(j + 1) * P],
                                                  feat[:, k, :], start=(k == 0), stop=(k == K - 1))
                        mm.then_inc(u_done, 1)
                def add_to_v(g, k):
                    h, b = g // DB, g % DB
                    for part in range(2):
                        mm = nc.tensor.matmul(banks[g][:, :], mid[:, k, part * D + b * P:part * D + (b + 1) * P],
                                              HT[:, k, h * BANK:(h + 1) * BANK],
                                              start=(k == 0 and part == 0), stop=(k == K - 1 and part == 1))
                    if k == K - 1:
                        mm.then_inc(v_done, 1)

                if first:
                    for k in range(K):
                        if k == K - 1:
                            pe.wait_ge(beta_set, HB)
                            for b in range(HB):
                                mm = nc.tensor.matmul(banks[6][:, 0:D], beta_cols[:, b, :], w2[:, b, :],
                                                      start=(b == 0), stop=(b == HB - 1))
                            mm.then_inc(bw_done, 1)
                        pe.wait_ge(u_hi, n * K + k + 1)
                        pe.wait_ge(u_lo, n * K + k + 1)
                        for g in range(min(k, DB * CH)):
                            add_to_v(g, k)
                        if k < DB * CH:
                            for earlier in range(k + 1):
                                add_to_v(k, earlier)
                else:
                    for g in range(DB * CH):
                        for k in range(K):
                            if g == 0:
                                pe.wait_ge(u_hi, n * K + k + 1)
                                pe.wait_ge(u_lo, n * K + k + 1)
                            add_to_v(g, k)
                for step in range(K + Q_LAG):
                    j = step
                    if j < K:
                        if first and 4 + j == 6:
                            pe.wait_ge(bw_set, 1)
                        if j % 4 == 0:
                            pe.wait_ge(v_set, n * DB * CH + (j // 4 + 1) * DB)
                        if j >= 4:
                            pe.wait_ge(z_set, n * K + j - 3)
                        for b in range(DB):
                            mm = nc.tensor.matmul(banks[4 + j % 4][:, :], vT[:, b, j * P:(j + 1) * P],
                                                  w1[:, b, :], start=(b == 0), stop=(b == DB - 1))
                        mm.then_inc(z_done, 1)
                    j = step - T_LAG
                    if 0 <= j < K:
                        pe.wait_ge(t_set, n * K + j + 1)
                        if j >= 2:
                            pe.wait_ge(tT_set, n * K + j - 1)
                        for b in range(HB):
                            mm = nc.tensor.transpose(banks[j % 2][:, b * P:(b + 1) * P],
                                                     hid[:, j, b * P:(b + 1) * P], ident[:])
                        mm.then_inc(tT_done, 1)
                    j = step - Q_LAG
                    if 0 <= j:
                        pe.wait_ge(tT_set, n * K + j + 1)
                        if first and j == 0:
                            pe.wait_ge(w2_scaled, HB)
                        if 2 <= j < 6:
                            pe.wait_ge(z_set, n * K + j + 3)
                        elif j >= 6:
                            pe.wait_ge(q_whole, n * K + j - 5)
                        for b in range(HB):
                            mm = nc.tensor.matmul(banks[Q_BANK[j]][:, 0:D], hidT[:, j % 2, b, :], w2[:, b, :],
                                                  start=(b == 0), stop=(b == HB - 1))
                        mm.then_inc(q_done, 1)
                for j, blocks in P_ORDER:
                    for k in blocks:
                        if j < 2:
                            pe.wait_ge(q_lo, n * K + k + 1)
                        mm = nc.tensor.matmul(banks[(4 + j) % 8][:, :], H[:, k, j * P:(j + 1) * P],
                                              feat[:, k, :], start=(k == 0), stop=(k == K - 1))
                        if k == K - 1:
                            mm.then_inc(p_done, 1)
                for j, blocks in P_ORDER:
                    for k in blocks:
                        if j < 2:
                            pe.wait_ge(p_lo, n * K + k + 1)
                        if k == 0 and j < 4:
                            pe.wait_ge(p_whole, n * K + 5 + j)
                        mm = nc.tensor.matmul(banks[j][:, :], HT[:, k, j * P:(j + 1) * P],
                                              mid[:, k, :], start=(k == 0), stop=(k == K - 1))
                        if k == K - 1:
                            mm.then_inc(s_done, 1)

            over_graphs(pe, graph)


def kernel(**inputs):
    import numpy as np
    import concourse.bacc as bacc
    from concourse.bass_utils import run_bass_kernel_spmd

    laid_out = {
        "x": inputs["x"], "adj": inputs["adj"],
        "w1t": np.asarray(inputs["L0_gnn_W1"]).T, "b1": inputs["L0_gnn_b1"],
        "gamma": np.asarray(inputs["L0_gnn_gamma"]).reshape(-1, P).T,
        "beta": np.asarray(inputs["L0_gnn_beta"]).reshape(-1, P).T,
        "w2t": np.asarray(inputs["L0_gnn_W2"]).T, "b2": inputs["L0_gnn_b2"],
    }
    nc = bacc.Bacc("TRN2", target_bir_lowering=False, num_devices=1)
    arrays, args = {}, []
    for name, value in laid_out.items():
        a = np.ascontiguousarray(value)
        arrays[f"in_{name}"] = a
        args.append(nc.dram_tensor(f"in_{name}", a.shape, mybir.dt.from_np(a.dtype), kind="ExternalInput").ap())
    shape = arrays["in_x"].shape
    args.append(nc.dram_tensor("out_0", shape, F32, kind="ExternalOutput").ap())
    graph_kernel(nc, *args)
    result = run_bass_kernel_spmd(nc, [arrays], core_ids=[0])
    return result.results[0]["out_0"]
```
